# Optimizing a Trainium2 kernel written in Bass

```python
import numpy as np
import jax
import jax.numpy as jnp

def _softmax(x, axis=-1):
    return jax.nn.softmax(x, axis=axis)

def _gelu(x):
    return jax.nn.gelu(x, approximate=True)

def _silu(x):
    return jax.nn.silu(x)

def _sigmoid(x):
    return jax.nn.sigmoid(x)

def _layernorm(x, axis=-1, eps=1e-05):
    m = jnp.mean(x, axis=axis, keepdims=True)
    v = jnp.var(x, axis=axis, keepdims=True)
    return (x - m) / jnp.sqrt(v + eps)

def _scatter_add(tgt, idx, src, axis=0):
    return tgt.at[idx].add(src)

def _segment_sum(src, seg, n):
    return jax.ops.segment_sum(src, seg, n)
kernel_name = 'mk_xattn_ffn_d1_seqx_r2_e02f20'

def setup_inputs(seed: int=0):
    np.random.seed(seed)
    _w = jnp.asarray

    def _rec_inputs():
        import jax
        import jax.numpy as jnp
        _rk = jax.random.key(seed)
        x = 0.01048 + 0.1018 * jax.random.normal(jax.random.fold_in(_rk, 1), (4, 1024, 1024), jnp.float32)
        _lenS = 1024 - jax.random.randint(jax.random.fold_in(_rk, 7), (4,), 0, max(1, 1024 // 4) + 1, jnp.int32)
        _lenS2 = 1024 - jax.random.randint(jax.random.fold_in(_rk, 8), (4,), 0, max(1, 1024 // 4) + 1, jnp.int32)
        _ctx_512P = jax.random.normal(jax.random.fold_in(_rk, 11), (4, 16, 256), jnp.float32)
        _ctx_512c = jax.random.dirichlet(jax.random.fold_in(_rk, 511), 0.3 * jnp.ones((16,), jnp.float32), (4, 1024))
        _ctx_512t = jnp.einsum('bsk,bkd->bsd', _ctx_512c, _ctx_512P)
        _ctx_512t = _ctx_512t * jax.lax.rsqrt(jnp.mean(jnp.square(_ctx_512t)) + 1e-12) * 0.953939
        ctx_512 = -0.000292821 + 1.00034 * (_ctx_512t + 0.3 * jax.random.normal(jax.random.fold_in(_rk, 611), (4, 1024, 256), jnp.float32))
        return (x, ctx_512)
    x, ctx_512 = _rec_inputs()

    def _L0_xattn_setup():
        import jax, jax.numpy as jnp
        import numpy as np
        LRELU_ALPHA = 0.2
        MASK_VAL = -10000000000.0
        B, N, F_IN = (4, 1024, 256)
        H, F_OUT = (8, 128)
        F_HID = H * F_OUT

        def gat_layer(x, adj, W, a_self, a_neigh, b):
            feat = jnp.einsum('nf,hfo->hno', x, W)
            attn_self = jnp.einsum('hno,ho->hn', feat, a_self)
            attn_neigh = jnp.einsum('hno,ho->hn', feat, a_neigh)
            e = attn_self[:, :, None] + attn_neigh[:, None, :]
            e = jax.nn.leaky_relu(e, LRELU_ALPHA)
            e = e + MASK_VAL * (1.0 - adj)[None, :, :]
            alpha = jax.nn.softmax(e, axis=-1)
            out = jnp.einsum('hnm,hmo->hno', alpha, feat) + b[:, None, :]
            out = jnp.transpose(out, (1, 0, 2)).reshape(out.shape[1], -1)
            return jax.nn.elu(out)
        key = jax.random.key(seed)
        ks = jax.random.split(key, 10)
        feats = jax.random.normal(ks[0], (B, N, F_IN), dtype=jnp.float32)
        a = (jax.random.uniform(ks[1], (B, N, N)) < 0.01).astype(jnp.float32)
        adj = jnp.maximum(a, jnp.eye(N, dtype=jnp.float32)[None])
        s0 = 1.0 / np.sqrt(F_IN)
        s1 = 1.0 / np.sqrt(F_HID)
        return {'feats': feats, 'adj': adj, 'W0': jax.random.normal(ks[2], (H, F_IN, F_OUT), dtype=jnp.float32) * s0, 'a_self0': jax.random.normal(ks[3], (H, F_OUT), dtype=jnp.float32) * 0.1, 'a_neigh0': jax.random.normal(ks[4], (H, F_OUT), dtype=jnp.float32) * 0.1, 'b0': jnp.zeros((H, F_OUT), dtype=jnp.float32), 'W1': jax.random.normal(ks[5], (H, F_HID, F_OUT), dtype=jnp.float32) * s1, 'a_self1': jax.random.normal(ks[6], (H, F_OUT), dtype=jnp.float32) * 0.1, 'a_neigh1': jax.random.normal(ks[7], (H, F_OUT), dtype=jnp.float32) * 0.1, 'b1': jnp.zeros((H, F_OUT), dtype=jnp.float32)}
    _L0_xattn_all = _L0_xattn_setup()
    _L0_xattn_in = {k: v for k, v in _L0_xattn_all.items() if k in ('W0', 'a_self0', 'a_neigh0', 'b0', 'W1', 'a_self1', 'a_neigh1', 'b1')}
    del _L0_xattn_all

    def _L0_ffn_setup():
        import jax, jax.numpy as jnp
        import numpy as np
        B, S, D = (4, 2048, 1024)
        DFF = 4 * D
        SKIP = 0.125
        key = jax.random.key(seed)
        ks = jax.random.split(key, 4)
        s_in = 1.0 / np.sqrt(D).astype(np.float32)
        s_ff = 1.0 / np.sqrt(DFF).astype(np.float32)
        return {'x': jax.random.normal(ks[0], (B, S, D), jnp.float32), 'Wr': jax.random.normal(ks[1], (D, 1), jnp.float32) * s_in, 'br': jnp.zeros((1,), jnp.float32), 'W1': jax.random.normal(ks[2], (D, DFF), jnp.float32) * s_in, 'b1': jnp.zeros((DFF,), jnp.float32), 'W2': jax.random.normal(ks[3], (DFF, D), jnp.float32) * s_ff, 'b2': jnp.zeros((D,), jnp.float32)}
    _L0_ffn_all = _L0_ffn_setup()
    _L0_ffn_in = {k: v for k, v in _L0_ffn_all.items() if k in ('Wr', 'br', 'W1', 'b1', 'W2', 'b2')}
    del _L0_ffn_all
    return {'x': x, 'ctx_512': ctx_512, 'L0_xattn_W0': _L0_xattn_in['W0'], 'L0_xattn_a_self0': _L0_xattn_in['a_self0'], 'L0_xattn_a_neigh0': _L0_xattn_in['a_neigh0'], 'L0_xattn_b0': _L0_xattn_in['b0'], 'L0_xattn_W1': _L0_xattn_in['W1'], 'L0_xattn_a_self1': _L0_xattn_in['a_self1'], 'L0_xattn_a_neigh1': _L0_xattn_in['a_neigh1'], 'L0_xattn_b1': _L0_xattn_in['b1'], 'L0_ffn_Wr': _L0_ffn_in['Wr'], 'L0_ffn_br': _L0_ffn_in['br'], 'L0_ffn_W1': _L0_ffn_in['W1'], 'L0_ffn_b1': _L0_ffn_in['b1'], 'L0_ffn_W2': _L0_ffn_in['W2'], 'L0_ffn_b2': _L0_ffn_in['b2']}

def reference(x, ctx_512, L0_xattn_W0, L0_xattn_a_self0, L0_xattn_a_neigh0, L0_xattn_b0, L0_xattn_W1, L0_xattn_a_self1, L0_xattn_a_neigh1, L0_xattn_b1, L0_ffn_Wr, L0_ffn_br, L0_ffn_W1, L0_ffn_b1, L0_ffn_W2, L0_ffn_b2):
    import jax
    import jax.numpy as jnp

    def _L0_xattn_ref(feats, adj, W0, a_self0, a_neigh0, b0, W1, a_self1, a_neigh1, b1):
        import jax, jax.numpy as jnp
        import numpy as np
        LRELU_ALPHA = 0.2
        MASK_VAL = -10000000000.0
        B, N, F_IN = (4, 1024, 256)
        H, F_OUT = (8, 128)
        F_HID = H * F_OUT

        def gat_layer(x, adj, W, a_self, a_neigh, b):
            feat = jnp.einsum('nf,hfo->hno', x, W)
            attn_self = jnp.einsum('hno,ho->hn', feat, a_self)
            attn_neigh = jnp.einsum('hno,ho->hn', feat, a_neigh)
            e = attn_self[:, :, None] + attn_neigh[:, None, :]
            e = jax.nn.leaky_relu(e, LRELU_ALPHA)
            e = e + MASK_VAL * (1.0 - adj)[None, :, :]
            alpha = jax.nn.softmax(e, axis=-1)
            out = jnp.einsum('hnm,hmo->hno', alpha, feat) + b[:, None, :]
            out = jnp.transpose(out, (1, 0, 2)).reshape(out.shape[1], -1)
            return jax.nn.elu(out)

        def per_graph(x, a):
            h = gat_layer(x, a, W0, a_self0, a_neigh0, b0)
            return gat_layer(h, a, W1, a_self1, a_neigh1, b1)
        return jax.vmap(per_graph)(feats, adj)

    def _L0_ffn_ref(x, Wr, br, W1, b1, W2, b2):
        import jax, jax.numpy as jnp
        import numpy as np
        B, S, D = (4, 2048, 1024)
        DFF = 4 * D
        SKIP = 0.125
        Bs, Ss, Ds = x.shape
        k = max(int(Ss * SKIP), 1)
        logits = (x @ Wr + br)[..., 0]
        weights, idx = jax.lax.top_k(logits, k)
        perm = jnp.argsort(idx, axis=1)
        tokens = jnp.take_along_axis(idx, perm, axis=1)
        fx = jnp.take_along_axis(x, tokens[..., None], axis=1)
        h = jax.nn.gelu(fx @ W1 + b1, approximate=False)
        out_l = h @ W2 + b2
        tw = jax.nn.softmax(weights, axis=1)
        rw = jnp.take_along_axis(tw, perm, axis=1)
        xw = rw[..., None] * out_l
        bidx = jnp.arange(Bs)[:, None]
        return x.at[bidx, tokens].add(xw)
    x = x + _L0_xattn_ref(ctx_512, _layernorm(x, axis=-1), L0_xattn_W0, L0_xattn_a_self0, L0_xattn_a_neigh0, L0_xattn_b0, L0_xattn_W1, L0_xattn_a_self1, L0_xattn_a_neigh1, L0_xattn_b1)
    x = x + _L0_ffn_ref(_layernorm(x, axis=-1), L0_ffn_Wr, L0_ffn_br, L0_ffn_W1, L0_ffn_b1, L0_ffn_W2, L0_ffn_b2)
    return x

_drawn_inputs = setup_inputs


def setup_inputs(seed=0):
    import zlib

    import numpy as np

    out = dict(_drawn_inputs(seed))
    spreads = {'L0_xattn_b0': (0.0, 0.1),
     'L0_xattn_b1': (0.0, 0.1),
     'L0_ffn_b1': (0.0, 0.8),
     'L0_ffn_b2': (0.0, 0.8)}
    factors = {'L0_ffn_Wr': 8.0, 'L0_ffn_W1': 8.0, 'L0_ffn_W2': 8.0}
    for name, (base, spread) in spreads.items():
        noise = np.random.default_rng([zlib.crc32(name.encode()), seed]).standard_normal(out[name].shape)
        drawn = base * np.exp(spread * noise) if base else spread * noise
        out[name] = jnp.asarray(drawn.astype(out[name].dtype))
    for name, factor in factors.items():
        out[name] = (out[name] * factor).astype(out[name].dtype)
    return out
```

```python
from contextlib import ExitStack

import concourse.bass as bass
from concourse import mybir

F32 = mybir.dt.float32
F32R = mybir.dt.float32r
I32 = mybir.dt.int32
U32 = mybir.dt.uint32
ALU = mybir.AluOpType
ACT = mybir.ActivationFunctionType
AX = mybir.AxisListType

P = 128
B, N, D = 4, 1024, 1024
FI = 256
H, FO = 8, 128
FF = 4096
TOP = N // 8
NT = N // P
KI = FI // P
KD = D // P
HALF = 512
NV = 5
GROUP = 256
GT = GROUP // P
NQ = N // GROUP
SLOTS = 2 * NT
GS = 2 * GT
NF = FF // P
FG = 4
MASK = -1.0e10
LRELU = 0.2
EPS = 1e-5
RSQRT_MAGIC = float(0x5F3759DF)
PARTS = [(0, 0), (0, 1), (1, 0)]
ROUNDINGS = 6.5e-7
UNDERFLOW = 200.0


LOOP_STEPS = 155
MASK_STEPS, FEAT_STEPS, HEAD_STEPS, ROW_STEPS, END_STEPS = 24, 8, 11, 8, 94
LAYER_STEPS = NT * FEAT_STEPS + H * (HEAD_STEPS + NT * ROW_STEPS)


class Names:
    pass


class Count:

    def __init__(self, sem):
        self.sem, self.base, self.n, self.loops = sem, 0, 0, []

    def inc(self, instruction):
        self.n += 1
        return instruction.then_inc(self.sem, 1)

    def value(self):
        return self.base + self.n

    def enter(self, i, first, each):
        self.loops.append((self.base, self.n, each))
        self.base, self.n = (i - first) * each + (self.base + self.n), 0

    def leave(self, turns):
        self.base, n, each = self.loops.pop()
        assert self.n == each, (self.n, each)
        self.n = n + turns * each


def rsqrt(dve, step, v, y, t):
    step(dve.tensor_scalar(y.bitcast(I32), v.bitcast(I32), -0.5, RSQRT_MAGIC, ALU.mult, ALU.add))
    for _ in range(4):
        step(dve.tensor_tensor(t, y, v, ALU.mult))
        step(dve.tensor_tensor(t, t, y, ALU.mult))
        step(dve.tensor_scalar(t, t, -0.5, 1.5, ALU.mult, ALU.add))
        step(dve.tensor_tensor(y, y, t, ALU.mult))


def make_constants(sb, sem):
    k = Names()
    k.ident = sb("ident", [P, P])
    k.ones = sb("ones", [P, P])
    k.below = sb("below", [P, P])
    k.slot_i = sb("slot_i", [P, P], I32)
    k.slot = sb("slot", [P, P])
    k.row_i = sb("row_i", [P, NT], I32)
    k.row = sb("row", [P, NT])
    pool_made, dve_made = sem("pool_made"), sem("dve_made")

    def pool(e):
        e.memset(k.ident[:], 1.0).then_inc(pool_made, 1)
        e.memset(k.ones[:], 1.0).then_inc(pool_made, 1)
        e.memset(k.below[:], 1.0).then_inc(pool_made, 1)
        e.wait_ge(pool_made, 3)
        e.affine_select(out=k.ident[:], in_=k.ident[:], compare_op=ALU.is_equal, fill=0.0, base=0,
                        pattern=[[1, P]], channel_multiplier=-1).then_inc(pool_made, 1)
        e.affine_select(out=k.below[:], in_=k.below[:], compare_op=ALU.is_gt, fill=0.0, base=0,
                        pattern=[[-1, P]], channel_multiplier=1).then_inc(pool_made, 1)
        e.iota(k.slot_i[:], [[1, P]], base=0, channel_multiplier=0).then_inc(pool_made, 1)
        e.iota(k.row_i[:], [[P, NT]], base=0, channel_multiplier=1).then_inc(pool_made, 1)
    k.pool = pool

    def dve(e):
        e.wait_ge(pool_made, 7)
        e.tensor_copy(k.slot[:], k.slot_i[:]).then_inc(dve_made, 1)
        e.tensor_copy(k.row[:], k.row_i[:]).then_inc(dve_made, 1)
        e.wait_ge(dve_made, 2)
    k.dve = dve

    def pe(e):
        e.wait_ge(dve_made, 2)
    k.pe = pe
    return k



def make_ending(nc, sb, big, late, sem, k, a, out, feat_dram, ps):
    s = Names()
    s.index = sb("index", [P, NT], U32)
    s.row = sb("row_now", [P, NT])
    s.wr_sum = sb("wr_sum", [P, 1])
    s.br = sb("br", [P, 1])
    s.bn = sb("bn", [P, 2, 2, 6])
    s.stats = sb("stats", [P, NT, 2])
    s.dot = sb("dot", [P, NT])
    s.var = sb("var", [P, NT])
    s.rstd = sb("rstd", [P, NT])
    s.tmp = sb("tmp", [P, NT])
    s.scale = sb("scale", [P, NT])
    s.shift = sb("shift", [P, NT])
    s.values = sb("values", [P, NT, NV])
    s.ranks = sb("ranks", [P, NT, 4])
    s.rank = sb("rank", [P, NT])
    s.same = sb("same", [P, P])
    s.chosen = sb("chosen", [P, B * NV])
    s.token = sb("token", [P, B, 2], U32)
    s.weight = sb("weight", [P, B])
    with ExitStack() as place:
        s.w2s = [late(place, "fw2_hi", [P, FG, D], F32R), late(place, "fw2_lo", [P, FG, D], F32R)]
    s.x1 = big("x1", [P, NT, D])
    s.xin = big("xin", [P, 2, D])
    s.wr = big("wr", [P, D])
    s.diag = big("diag", [P, NT, P])
    spread_ps = ps[:, 5:7].rearrange("p a b -> p (a b)")
    s.products = spread_ps
    counted = s.diag[:].rearrange("p t c -> p (t c)")
    pick_ps = ps[:, 7, 0:NV]

    s.x_in = [sem("x_in0"), sem("x_in1")]
    s.feat_in = sem("feat_in")
    s.x1_made = sem("x1_made")
    s.base_made = sem("base_made")
    s.base_out = sem("base_out")
    s.consts_in = sem("consts_in")
    s.diag_made = sem("diag_made")
    s.spread = sem("spread")
    s.onehot_made = sem("onehot_made")
    s.picked = sem("picked")
    s.v = Count(sem("dve_step"))

    def done(ins):
        s.v.inc(ins)
        nc.vector.wait_ge(s.v.sem, s.v.value())
    s.done = done

    def sp_consts(e):
        e.dma_start(s.wr[:], a.wr.to_broadcast([P, D])).then_inc(s.consts_in, 16)
        e.dma_start(s.br[:], a.br.rearrange("(a o) -> a o", a=1).to_broadcast([P, 1])).then_inc(s.consts_in, 16)
    s.sp_consts = sp_consts

    def dve_consts(e):
        e.wait_ge(s.consts_in, 32)
        done(e.reduce_sum(s.wr_sum[:], s.wr[:], axis=AX.X))
        done(e.memset(s.ranks[:], 0.0))
        done(e.tensor_copy(s.row[:], k.row[:]))
    s.dve_consts = dve_consts

    def sp_tile(e, b, t, first=False):
        if not first:
            e.wait_ge(s.x1_made, b * NT + t - 1)
        e.dma_start(s.xin[:, t % 2], a.x[bass.ds((b * NT + t) * P, P), :]).then_inc(s.x_in[t % 2], 16)
    s.sp_tile = sp_tile

    def pool_gather(e, b, t):
        e.indirect_dma_start(out=s.x1[:, t].bitcast(U32), out_offset=None, in_=feat_dram,
                             in_offset=bass.IndirectOffsetOnAxis(ap=s.index[:, t:t + 1], axis=0),
                             ).then_inc(s.feat_in, 16)
    s.pool_gather = pool_gather

    def pool_add(e, b, t):
        e.wait_ge(s.x_in[t % 2], b * (NT // 2 * 16) + (t // 2 + 1) * 16)
        e.wait_ge(s.feat_in, (b * NT + NT) * 16)
        e.tensor_tensor(s.x1[:, t], s.x1[:, t], s.xin[:, t % 2], ALU.add).then_inc(s.x1_made, 1)
    s.pool_add = pool_add

    def dve_tile(e, b, t):
        e.wait_ge(s.x1_made, b * NT + t + 1)
        for h in range(2):
            s.v.inc(e.bn_stats(s.bn[:, t % 2, h], s.x1[:, t, h * HALF:(h + 1) * HALF]))
        e.wait_ge(s.v.sem, s.v.value())
        s.v.inc(e.tensor_tensor_reduce(out=s.products, in0=s.x1[:, t], in1=s.wr[:], scale=1.0, scalar=0.0,
                                       op0=ALU.mult, op1=ALU.add, accum_out=s.dot[:, t:t + 1]))
        done(e.bn_aggr(s.stats[:, t], s.bn[:, t % 2].rearrange("p h s -> p (h s)")))
    s.dve_tile = dve_tile

    def dve_norm(e, b):
        mean = s.stats[:, :, 0]
        done(e.tensor_scalar(s.var[:], s.stats[:, :, 1], EPS, None, ALU.add))
        rsqrt(e, done, s.var[:], s.rstd[:], s.tmp[:])
        done(e.tensor_scalar(s.scale[:], s.rstd[:], 1.0, None, ALU.add))
        done(e.tensor_tensor(s.tmp[:], mean, s.rstd[:], ALU.mult))
        done(e.tensor_scalar(s.shift[:], s.tmp[:], -1.0, None, ALU.mult))
        done(e.tensor_scalar(s.tmp[:], mean, s.wr_sum[:, 0:1], -1.0, ALU.mult, ALU.mult))
        done(e.tensor_tensor(s.tmp[:], s.tmp[:], s.dot[:], ALU.add))
        done(e.tensor_tensor(s.tmp[:], s.tmp[:], s.rstd[:], ALU.mult))
        done(e.tensor_scalar(s.values[:, :, 1], s.tmp[:], s.br[:, 0:1], None, ALU.add))
        s.v.inc(e.tensor_copy(s.values[:, :, 0], s.row[:]))
        s.v.inc(e.tensor_copy(s.values[:, :, 2], s.index[:]))
        s.v.inc(e.tensor_copy(s.values[:, :, 3], mean))
        s.v.inc(e.tensor_copy(s.values[:, :, 4], s.rstd[:]))
        e.wait_ge(s.v.sem, s.v.value())
        done(e.tensor_scalar(s.row[:], s.row[:], float(N), None, ALU.add))
        for t in range(NT):
            e.tensor_scalar(s.diag[:, t], k.ident[:], s.values[:, t, 1:2], None, ALU.mult).then_inc(s.diag_made, 1)
    s.dve_norm = dve_norm

    def act_base(e, b, t):
        e.wait_ge(s.diag_made, b * NT + NT)
        e.activation(s.x1[:, t], s.x1[:, t], ACT.Identity, scale=s.scale[:, t:t + 1],
                     bias=s.shift[:, t:t + 1]).then_inc(s.base_made, 1)
    s.act_base = act_base

    def sp_base(e, b, t):
        e.wait_ge(s.base_made, b * NT + t + 1)
        e.dma_start(out[bass.ds((b * NT + t) * P, P), :], s.x1[:, t]).then_inc(s.base_out, 16)
    s.sp_base = sp_base

    def pe_spread(e, b):
        e.wait_ge(s.diag_made, b * NT + NT)
        for t in range(NT):
            ins = e.matmul(spread_ps[:, t * P:(t + 1) * P], k.ones[:], s.diag[:, t], start=True, stop=True)
        ins.then_inc(s.spread, 1)
    s.pe_spread = pe_spread

    def dve_rank(e, b, t):
        if t == 0:
            e.wait_ge(s.spread, b + 1)
        own, at = s.values[:, t, 1:2], t * P
        if t:
            s.v.inc(e.tensor_scalar(counted[:, 0:at], spread_ps[:, 0:at], own, 0.0, ALU.is_ge, ALU.add,
                                    accum_out=s.ranks[:, t, 0:1]))
        if t < NT - 1:
            s.v.inc(e.tensor_scalar(counted[:, at + P:], spread_ps[:, at + P:], own, 0.0, ALU.is_gt, ALU.add,
                                    accum_out=s.ranks[:, t, 1:2]))
        s.v.inc(e.tensor_scalar(counted[:, at:at + P], spread_ps[:, at:at + P], own, 0.0, ALU.is_gt, ALU.add,
                                accum_out=s.ranks[:, t, 2:3]))
        done(e.scalar_tensor_tensor(out=s.same[:], in0=spread_ps[:, at:at + P], scalar=own, in1=k.below[:],
                                    op0=ALU.is_equal, op1=ALU.mult, accum_out=s.ranks[:, t, 3:4]))
    s.dve_rank = dve_rank

    def dve_onehot(e, b):
        done(e.reduce_sum(s.rank[:], s.ranks[:], axis=AX.X))
        for t in range(NT):
            e.tensor_scalar(s.diag[:, t], k.slot[:], s.rank[:, t:t + 1], None,
                            ALU.is_equal).then_inc(s.onehot_made, 1)
    s.dve_onehot = dve_onehot

    def pe_pick(e, b):
        e.wait_ge(s.onehot_made, b * NT + NT)
        for t in range(NT):
            ins = e.matmul(pick_ps, s.diag[:, t], s.values[:, t], start=(t == 0), stop=(t == NT - 1))
        ins.then_inc(s.picked, 1)
    s.pe_pick = pe_pick

    def dve_chosen(e, b):
        e.wait_ge(s.picked, b + 1)
        done(e.tensor_copy(s.chosen[:, bass.ds(b * NV, NV)], pick_ps))
    s.dve_chosen = dve_chosen
    return s


def make_ffn(nc, big, sem, k, s, a, out, feat_dram, ps):
    f = Names()
    NTOK = B * TOP
    NO = 2 * B
    NGRP = NF // FG
    fx = big("fx", [P, B, D])
    acc = fx
    rows = big("rows", [P, B, D])
    fxT = [big("fxT_hi", [P, KD, NTOK], F32R), big("fxT_lo", [P, KD, NTOK], F32R)]
    w1 = big("fw1", [P, FG, KD, P])
    w1s = [big("fw1_hi", [P, 2, KD, P], F32R), big("fw1_lo", [P, 2, KD, P], F32R)]
    w2 = big("fw2", [P, FG, D])
    hid = big("hid", [P, 2, NTOK])
    hids = [big("hid_hi", [P, FG, NTOK], F32R), big("hid_lo", [P, FG, NTOK], F32R)]
    b2 = big("fb2", [P, D])
    w2s = s.w2s
    b1 = big("fb1", [P, NF])
    wl = big("wl", [P, P])
    soft = big("soft", [P, 4])
    tok_in = sem("tok_in")
    fx_made, fx_turned = sem("fx_made"), sem("fx_turned")
    fx_hi, fx_lo = sem("fx_hi"), sem("fx_lo")
    w1_in = [sem(f"w1_in{i}") for i in range(FG)]
    w2_in = [sem(f"w2_in{i}") for i in range(FG)]
    w1_hi, w1_lo, w2_hi, w2_lo = sem("w1_hi"), sem("w1_lo"), sem("w2_hi"), sem("w2_lo")
    up_made, gelu, hid_hi, hid_lo = sem("up_made"), sem("gelu"), sem("hid_hi"), sem("hid_lo")
    down_made, added, row_made = sem("down_made"), sem("added"), sem("row_made")
    scattered, bias_in, tok_made = sem("scattered"), sem("bias_in"), sem("tok_made")
    wl_turned, wl_soft, wl_exp, wl_back = sem("wl_turned"), sem("wl_soft"), sem("wl_exp"), sem("wl_back")
    w1_src = a.fw1.rearrange("(k p) f -> p k f", p=P)
    v, done = s.v, s.done

    def groups(e, turn):
        turn(0, True)
        with e.Fori(1, NGRP) as i:
            turn(i, False)

    def sp_biases(e):
        with nc.allow_non_contiguous_dma(reason="the bias by partition, 16 KB"):
            e.dma_start(b1[:], a.fb1.rearrange("(c p) -> p c", p=P)).then_inc(bias_in, 16)
        e.dma_start(b2[:], a.fb2.rearrange("(a d) -> a d", a=1).to_broadcast([P, D])).then_inc(bias_in, 16)

    def sp(e):
        def turn(i, first):
            for j in range(FG):
                c = i * FG + j
                if not first:
                    e.wait_ge(w1_hi, c - FG + 1)
                    e.wait_ge(w1_lo, c - FG + 1)
                e.dma_start(w1[:, j], w1_src[:, :, bass.ds(c * P, P)]).then_inc(w1_in[j], 16)
                if not first:
                    e.wait_ge(w2_hi, c - FG + 1)
                    e.wait_ge(w2_lo, c - FG + 1)
                e.dma_start(w2[:, j], a.fw2[bass.ds(c * P, P), :]).then_inc(w2_in[j], 16)
                if first and j == 0:
                    sp_biases(e)
        groups(e, turn)
    f.sp = sp

    def pool(e):
        for b in range(B):
            e.wait_ge(tok_made, b + 1)
            e.indirect_dma_start(out=fx[:, b], out_offset=None, in_=a.x,
                                 in_offset=bass.IndirectOffsetOnAxis(ap=s.token[:, b, 0:1], axis=0)
                                 ).then_inc(tok_in, 16)
            e.indirect_dma_start(out=rows[:, b].bitcast(U32), out_offset=None, in_=feat_dram,
                                 in_offset=bass.IndirectOffsetOnAxis(ap=s.token[:, b, 1:2], axis=0)
                                 ).then_inc(tok_in, 16)
        e.wait_ge(s.base_out, B * NT * 16)
        for b in range(B):
            e.wait_ge(row_made, b + 1)
            e.indirect_dma_start(out=out, out_offset=bass.IndirectOffsetOnAxis(ap=s.token[:, b, 0:1], axis=0),
                                 in_=rows[:, b], in_offset=None).then_inc(scattered, 16)
        e.wait_ge(scattered, B * 16)
    f.pool = pool

    def dve_tokens(e):
        done(e.memset(wl[:], 0.0))
        for b in range(B):
            v.inc(e.tensor_copy(s.token[:, b, 0:1], s.chosen[:, b * NV:b * NV + 1]))
            v.inc(e.tensor_copy(s.token[:, b, 1:2], s.chosen[:, b * NV + 2:b * NV + 3]))
            e.wait_ge(v.sem, v.value())
            e.tensor_copy(wl[:, b:b + 1], s.chosen[:, b * NV + 1:b * NV + 2]).then_inc(tok_made, 1)

    def dve_rows(e, b):
        e.wait_ge(tok_in, 32 * B)
        at = b * NV
        done(e.tensor_tensor(rows[:, b], rows[:, b], fx[:, b], ALU.add))
        done(e.tensor_scalar(fx[:, b], rows[:, b], s.chosen[:, at + 3:at + 4], s.chosen[:, at + 4:at + 5],
                             ALU.subtract, ALU.mult))
        e.tensor_tensor(rows[:, b], rows[:, b], fx[:, b], ALU.add).then_inc(fx_made, 1)

    def w1_low(e, c, j, first):
        e.wait_ge(w1_hi, c + 1)
        if not first:
            e.wait_ge(up_made, c - 1)
        e.tensor_tensor(w1s[1][:, j % 2], w1[:, j], w1s[0][:, j % 2].bitcast(F32), ALU.subtract).then_inc(w1_lo, 1)

    def dve(e):
        dve_tokens(e)
        w1_low(e, 0, 0, True)
        w1_low(e, 1, 1, True)
        for b in range(B):
            dve_rows(e, b)
        for q in range(NO):
            b, c = q // 2, q % 2 * 4
            e.wait_ge(fx_hi, q + 1)
            e.tensor_tensor(fxT[1][:, c:c + 4, b * P:(b + 1) * P], ps[:, q % 4].rearrange("p (c j) -> p c j", c=4),
                            fxT[0][:, c:c + 4, b * P:(b + 1) * P].bitcast(F32), ALU.subtract).then_inc(fx_lo, 1)
        e.wait_ge(wl_turned, 1)
        done(e.tensor_reduce(soft[:, 0:1], ps[:, 4, 0:P], AX.X, ALU.max))
        e.tensor_scalar(soft[:, 1:2], soft[:, 0:1], -1.0, None, ALU.mult).then_inc(wl_soft, 1)
        e.wait_ge(wl_exp, 1)
        done(e.reciprocal(soft[:, 3:4], soft[:, 2:3]))
        e.tensor_scalar(wl[:], wl[:], soft[:, 3:4], None, ALU.mult).then_inc(wl_soft, 1)
        e.wait_ge(wl_back, 1)
        done(e.tensor_copy(s.weight[:], ps[:, 4, 0:B]))
        e.wait_ge(bias_in, 32)
        e.wait_ge(fx_turned, NO)
        for b in range(B):
            v.inc(e.tensor_copy(acc[:, b], b2[:]))
        e.wait_ge(v.sem, v.value())

        def w2_low(c, j, i, first):
            e.wait_ge(w2_hi, c + 1)
            if not first:
                e.wait_ge(down_made, i * NO)
            e.tensor_tensor(w2s[1][:, j], w2[:, j], w2s[0][:, j].bitcast(F32), ALU.subtract).then_inc(w2_lo, 1)

        def turn(i, first=False, last=False):
            for j in range(FG):
                c = i * FG + j
                w2_low(c, j, i, first)
                if j < FG - 2:
                    w1_low(e, c + 2, j + 2, False)
                e.wait_ge(hid_hi, c + 1)
                if not first:
                    e.wait_ge(down_made, i * NO)
                e.tensor_tensor(hids[1][:, j], hid[:, j % 2], hids[0][:, j].bitcast(F32),
                                ALU.subtract).then_inc(hid_lo, 1)
            if not last:
                for j in range(2):
                    w1_low(e, (i + 1) * FG + j, j, False)
            for o in range(NO):
                b, h = o // 2, o % 2
                e.wait_ge(down_made, i * NO + o + 1)
                if not first:
                    e.wait_ge(added, (i - 1) * NO + o + 1)
                e.tensor_tensor(acc[:, b, h * HALF:(h + 1) * HALF], acc[:, b, h * HALF:(h + 1) * HALF],
                                ps[:, 2 + o % 2], ALU.add).then_inc(added, 1)

        turn(0, first=True)
        with e.Fori(1, NGRP - 1) as i:
            turn(i)
        turn(NGRP - 1, last=True)
        for b in range(B):
            e.wait_ge(added, NGRP * NO)
            e.scalar_tensor_tensor(out=rows[:, b], in0=acc[:, b], scalar=s.weight[:, b:b + 1], in1=rows[:, b],
                                   op0=ALU.mult, op1=ALU.add).then_inc(row_made, 1)
    f.dve = dve

    def act(e):
        def w1_high(i, j, first=False):
            e.wait_ge(w1_in[j], (i + 1) * 16)
            if not first:
                e.wait_ge(up_made, i * FG + j - 1)
            e.activation(w1s[0][:, j % 2], w1[:, j], ACT.Copy).then_inc(w1_hi, 1)

        w1_high(0, 0, first=True)
        w1_high(0, 1, first=True)
        for q in range(NO):
            b, c = q // 2, q % 2 * 4
            e.wait_ge(fx_turned, q + 1)
            e.activation(fxT[0][:, c:c + 4, b * P:(b + 1) * P], ps[:, q % 4].rearrange("p (c j) -> p c j", c=4),
                         ACT.Copy).then_inc(fx_hi, 1)
        e.wait_ge(wl_soft, 1)
        e.activation(wl[:], ps[:, 4, 0:P], ACT.Exp, bias=soft[:, 1:2], accum_out=soft[:, 2:3]).then_inc(wl_exp, 1)
        e.wait_ge(bias_in, 32)
        e.wait_ge(s.base_out, B * NT * 16)

        def turn(i, first=False, last=False):
            for j in range(FG):
                c = i * FG + j
                e.wait_ge(w2_in[j], (i + 1) * 16)
                if not first:
                    e.wait_ge(down_made, i * NO)
                e.activation(w2s[0][:, j], w2[:, j], ACT.Copy).then_inc(w2_hi, 1)
                if j < FG - 2:
                    w1_high(i, j + 2)
                e.wait_ge(up_made, c + 1)
                if not (first and j < 2):
                    e.wait_ge(hid_lo, c - 1)
                e.activation(hid[:, j % 2], ps[:, j % 2], ACT.Gelu, bias=b1c(i, j)).then_inc(gelu, 1)
                e.wait_ge(gelu, c + 1)
                e.activation(hids[0][:, j], hid[:, j % 2], ACT.Copy).then_inc(hid_hi, 1)
            if not last:
                for j in range(2):
                    w1_high(i + 1, j)

        def b1c(i, j):
            return b1[:, i * FG + j:i * FG + j + 1] if isinstance(i, int) else b1[:, bass.ds(i * FG + j, 1)]

        turn(0, first=True)
        with e.Fori(1, NGRP - 1) as i:
            turn(i)
        turn(NGRP - 1, last=True)
    f.act = act

    def pe(e):
        e.wait_ge(tok_made, B)
        e.matmul(ps[:, 4, 0:P], wl[:], k.ident[:], start=True, stop=True).then_inc(wl_turned, 1)
        for q in range(NO):
            b, c0 = q // 2, q % 2 * 4
            e.wait_ge(fx_made, b + 1)
            if q >= 4:
                e.wait_ge(fx_lo, q - 3)
            for c in range(4):
                ins = e.transpose(ps[:, q % 4, c * P:(c + 1) * P], fx[:, b, (c0 + c) * P:(c0 + c + 1) * P], k.ident[:])
            ins.then_inc(fx_turned, 1)
        e.wait_ge(wl_soft, 2)
        e.matmul(ps[:, 4, 0:B], wl[:], k.ident[:, 0:B], start=True, stop=True).then_inc(wl_back, 1)
        e.wait_ge(fx_lo, NO)

        def turn(i, first):
            for j in range(FG):
                c = i * FG + j
                e.wait_ge(w1_lo, c + 1)
                if not (first and j < 2):
                    e.wait_ge(gelu, c - 1)
                for kk in range(KD):
                    for n, (w, x) in enumerate(PARTS):
                        ins = e.matmul(ps[:, j % 2], w1s[w][:, j % 2, kk], fxT[x][:, kk],
                                       start=(kk == 0 and n == 0), stop=(kk == KD - 1 and n == 2))
                ins.then_inc(up_made, 1)
            for o in range(NO):
                b, h = o // 2, o % 2
                if not (first and o < 2):
                    e.wait_ge(added, i * NO + o - 1)
                for j in range(FG):
                    if o == 0:
                        e.wait_ge(w2_lo, i * FG + j + 1)
                        e.wait_ge(hid_lo, i * FG + j + 1)
                    for n, (w, x) in enumerate(PARTS):
                        ins = e.matmul(ps[:, 2 + o % 2], hids[w][:, j, b * P:(b + 1) * P],
                                       w2s[x][:, j, h * HALF:(h + 1) * HALF],
                                       start=(j == 0 and n == 0), stop=(j == FG - 1 and n == 2))
                ins.then_inc(down_made, 1)
        groups(e, turn)
    f.pe = pe
    return f


def build_lead(nc, a, out, rows_dram, argmax_dram, flag):
    LEAD_AT = {t: t for t in range(NT)}
    TILE_AT = {4 + t: t for t in range(NT)}
    NORM_AT, PICK_AT = 12, 15
    RANK_AT = {13: range(0, 4), 14: range(4, NT)}
    INDEX_AT = 13
    LEADS_AT = 15
    BASE_AT = {13: range(0, 4), 14: range(4, NT)}
    Q_W0, Q_B0, Q_W1, Q_CTX, Q_A0, Q_A1, Q_LEAD = 0, 2, 3, 11, 12, 13, 14

    with ExitStack() as ctx:
        def sem(name):
            return ctx.enter_context(nc.semaphore(name))

        def maker(stack):
            return lambda name, shape, dt=F32: stack.enter_context(nc.sbuf_tensor(name, shape, dt))

        def late(stack, name, shape, dt):
            return stack.enter_context(nc.sbuf_tensor(name, shape, dt))

        ps = ctx.enter_context(nc.psum_tensor("ps", [P, 8, HALF], F32))
        small = maker(ctx)
        k = make_constants(small, sem)
        b0 = small("b0", [P, H])
        att = small("att", [2 * H, 2, FO])
        att_sq = small("att_sq", [P, FO])
        bounds = small("bounds", [P, P])
        total = small("total", [P, 2])
        q = small("q", [P, 16])
        lead_sq = small("lead_sq", [P, NT])
        top = small("top", [P, NT, 8])
        top_at = small("top_at", [P, NT, 8], U32)
        lead_row = small("lead_row", [P, 1])
        argmax_f = small("argmax_f", [P, NT])
        argmax = small("argmax", [P, NT], U32)
        l_var, l_rstd, l_tmp = small("l_var", [P, NT]), small("l_rstd", [P, NT]), small("l_tmp", [P, NT])
        l_gap, l_far, l_first = small("l_gap", [P, NT]), small("l_far", [P, 1]), small("l_first", [P, NT])
        ctx_sq = small("ctx_sq", [P, GT])
        ctx_max = small("ctx_max", [P, 1])
        lead_max = small("lead_max", [P, 1])

        s = make_ending(nc, small, small, late, sem, k, a, out, rows_dram, ps)
        v, done = s.v, s.done
        spread = s.diag
        with ExitStack() as layers:
            big = maker(layers)
            w0s = [big("w0_hi", [P, KI, D], F32R), big("w0_lo", [P, KI, D], F32R)]
            w1s = [big("w1_hi", [P, KD, D], F32R), big("w1_lo", [P, KD, D], F32R)]
            b1s = big("b1s", [P, D], F32R)
            b1_rows = big("b1_rows", [P, P], F32R)
            cx = big("cx", [P, GT, FI])
            cxT = [big("cxT_hi", [P, 2, KI, GROUP], F32R), big("cxT_lo", [P, 2, KI, GROUP], F32R)]
            hT = [big("hT_hi", [P, 2, KD, GROUP], F32R), big("hT_lo", [P, 2, KD, GROUP], F32R)]
            relu0, exp0 = big("relu0", [P, 2, GROUP]), big("exp0", [P, 4, GROUP])
            relu1 = big("relu1", [P, 2, HALF])
            y = big("y", [P, 2, D])
            xa = big("xa", [P, 2, D])
        ffn_ctx = ctx.enter_context(ExitStack())
        f = make_ffn(nc, maker(ffn_ctx), sem, k, s, a, out, rows_dram, ps)
        w0_raw, w1_raw = s.xin, s.x1
        b1_raw = s.diag[:].rearrange("p t c -> p (t c)")

        w_in = [sem("w0_in"), sem("w1_in_a"), sem("w1_in_b")]
        w0_hi, w0_lo, w1_hi, w1_lo = sem("lw0_hi"), sem("lw0_lo"), sem("lw1_hi"), sem("lw1_lo")
        b0_in, b1_in, b1_zero, b1_made = sem("b0_in"), sem("b1_in"), sem("b1_zero"), sem("b1_made")
        att_in = sem("att_in")
        cx_in, cx_turned, cx_hi, cx_lo = sem("cx_in"), sem("cx_turned"), sem("cx_hi"), sem("cx_lo")
        cx_squared = sem("cx_squared")
        l0_made, l0_acts, h_sum, h_high, h_lo = (sem(x) for x in ("l0_made", "l0_acts", "h_sum", "h_high", "h_lo"))
        l1_made, l1_acts, y_low, y_made = sem("l1_made"), sem("l1_acts"), sem("y_low"), sem("y_made")
        y_out = [sem("y_out0"), sem("y_out1")]
        xa_in = [sem("xa_in0"), sem("xa_in1")]
        xa_read, xa_squared, argmax_made, argmax_out = sem("xa_read"), sem("xa_squared"), sem("argmax_made"), sem("argmax_out")
        index_in, bound_made, bound_spread = sem("index_in"), sem("bound_made"), sem("bound_spread_made")


        def over_graphs(e, body):
            body(0, first=True)
            with e.Fori(1, B - 1) as b:
                body(b)
            body(B - 1, last=True)

        def pe_turn(e, g, first=False):
            e.wait_ge(cx_in, (g + 1) * 16)
            if not first:
                e.wait_ge(cx_lo, g)
            for r in range(GT):
                for c in range(KI):
                    ins = e.transpose(ps[:, 4, (c * GT + r) * P:(c * GT + r + 1) * P], cx[:, r, c * P:(c + 1) * P],
                                      k.ident[:])
            ins.then_inc(cx_turned, 1)

        def act_turned(e, g, u):
            e.wait_ge(cx_turned, g + 1)
            if not (isinstance(g, int) and g < 2):
                e.wait_ge(l0_made, (g - 1) * KD)
            e.activation(cxT[0][:, u], ps[:, 4].rearrange("p (c r) -> p c r", c=KI), ACT.Copy).then_inc(cx_hi, 1)

        def dve_turned(e, g, u):
            e.wait_ge(cx_hi, g + 1)
            e.tensor_tensor(cxT[1][:, u], ps[:, 4].rearrange("p (c r) -> p c r", c=KI),
                            cxT[0][:, u].bitcast(F32), ALU.subtract).then_inc(cx_lo, 1)

        def dve_squares(e, g):
            e.wait_ge(cx_in, (g + 1) * 16)
            if not (isinstance(g, int) and g == 0):
                e.wait_ge(cx_squared, g)
            for r in range(GT):
                done(e.tensor_tensor_reduce(out=ps[:, 7, FI:2 * FI], in0=cx[:, r], in1=cx[:, r],
                                            scale=1.0, scalar=0.0, op0=ALU.mult, op1=ALU.add,
                                            accum_out=ctx_sq[:, r:r + 1]))
            for r in range(GT):
                ins = e.tensor_tensor(ctx_max[:], ctx_max[:], ctx_sq[:, r:r + 1], ALU.max)
                if r < GT - 1:
                    done(ins)
            ins.then_inc(cx_squared, 1)

        def sp_ctx(e, g, first=False):
            if not first:
                e.wait_ge(cx_turned, g)
                e.wait_ge(cx_squared, g)
            e.dma_start(cx[:], a.ctx[bass.ds(g * GROUP, GROUP), :].rearrange("(r p) f -> p r f", p=P)
                        ).then_inc(cx_in, 16)

        def pe_layer0(e, g, c, u):
            n = g * KD + c
            if c == 0:
                e.wait_ge(cx_lo, g + 1)
            if not (isinstance(n, int) and n < 2):
                e.wait_ge(l0_acts, 2 * (n - 1))
            for kk in range(KI):
                for i, (w, x) in enumerate(PARTS):
                    ins = e.matmul(ps[:, c % 2, 0:GROUP], w0s[w][:, kk, c * P:(c + 1) * P], cxT[x][:, u, kk],
                                   start=(kk == 0 and i == 0), stop=(kk == KI - 1 and i == 2))
            ins.then_inc(l0_made, 1)

        def act_layer0(e, g, c):
            n = g * KD + c
            e.wait_ge(l0_made, n + 1)
            if not (isinstance(n, int) and n < 2):
                e.wait_ge(h_sum, n - 1)
            if not (isinstance(n, int) and n < 4):
                e.wait_ge(h_lo, n - 3)
            z = ps[:, c % 2, 0:GROUP]
            e.activation(relu0[:, c % 2], z, ACT.Relu, bias=b0[:, c:c + 1]).then_inc(l0_acts, 1)
            e.activation(exp0[:, c % 4], z, ACT.Exp, bias=b0[:, c:c + 1]).then_inc(l0_acts, 1)

        def dve_layer0(e, g, c, u):
            n = g * KD + c
            e.wait_ge(l0_acts, 2 * (n + 1))
            e.scalar_tensor_tensor(out=exp0[:, c % 4], in0=exp0[:, c % 4], scalar=1.0, in1=relu0[:, c % 2],
                                   op0=ALU.min, op1=ALU.add).then_inc(h_sum, 1)

        def act_high0(e, g, c, u):
            e.wait_ge(h_sum, g * KD + c + 1)
            if not (isinstance(g, int) and g < 2):
                e.wait_ge(l1_made, (g - 1) * GS)
            e.activation(hT[0][:, u, c], exp0[:, c % 4], ACT.Copy, bias=-1.0).then_inc(h_high, 1)

        def dve_low0(e, g, c, u):
            e.wait_ge(h_high, g * KD + c + 1)
            e.scalar_tensor_tensor(out=hT[1][:, u, c], in0=exp0[:, c % 4], scalar=-1.0,
                                   in1=hT[0][:, u, c].bitcast(F32), op0=ALU.add,
                                   op1=ALU.subtract).then_inc(h_lo, 1)

        def pe_layer1(e, b, S):
            g, r, h, u = b * NQ + S // GS, S // 2 % GT, S % 2, S // GS % 2
            n = b * SLOTS + S
            if S % GS == 0:
                e.wait_ge(h_lo, (g + 1) * KD)
            if not (isinstance(n, int) and n < 2):
                e.wait_ge(l1_acts, 2 * (n - 1))
            z = ps[:, 2 + h]
            cols = slice(h * HALF, (h + 1) * HALF)
            e.matmul(z, b1_rows[:], b1s[:, cols], start=True, stop=False)
            for kk in range(KD):
                for i, (w, x) in enumerate(PARTS):
                    ins = e.matmul(z, hT[w][:, u, kk, r * P:(r + 1) * P], w1s[x][:, kk, cols], start=False,
                                   stop=(kk == KD - 1 and i == 2))
            ins.then_inc(l1_made, 1)

        def act_layer1(e, b, S):
            n, h, r = b * SLOTS + S, S % 2, S // 2
            e.wait_ge(l1_made, n + 1)
            if not (isinstance(n, int) and n < 2):
                e.wait_ge(y_made, n - 1)
            e.activation(relu1[:, h], ps[:, 2 + h], ACT.Relu).then_inc(l1_acts, 1)
            if not (isinstance(b, int) and b * NT + r < 2):
                e.wait_ge(y_out[r % 2], b * (NT // 2 * 16) + r // 2 * 16)
            e.activation(y[:, r % 2, h * HALF:(h + 1) * HALF], ps[:, 2 + h], ACT.Exp).then_inc(l1_acts, 1)

        def dve_layer1(e, b, S):
            n, h, r = b * SLOTS + S, S % 2, S // 2
            e.wait_ge(l1_acts, 2 * (n + 1))
            yh = y[:, r % 2, h * HALF:(h + 1) * HALF]
            e.tensor_scalar(yh, yh, 1.0, -1.0, ALU.min, ALU.add).then_inc(y_low, 1)

        def pool_layer1(e, b, S):
            n, h, r = b * SLOTS + S, S % 2, S // 2
            e.wait_ge(y_low, n + 1)
            yh = y[:, r % 2, h * HALF:(h + 1) * HALF]
            e.tensor_tensor(yh, yh, relu1[:, h], ALU.add).then_inc(y_made, 1)

        def sp_rows(e, b, r):
            e.wait_ge(y_made, b * SLOTS + 2 * r + 2)
            e.dma_start(rows_dram[bass.ds((b * NT + r) * P, P), :], y[:, r % 2].bitcast(U32)).then_inc(y_out[r % 2], 16)

        def sp_lead(e, n, first=False, par=0):
            if not first:
                e.wait_ge(xa_squared, n - 1)
            e.dma_start(xa[:, par], a.x[bass.ds(n * P, P), :]).then_inc(xa_in[par], 16)

        def dve_lead(e, b, t):
            e.wait_ge(xa_in[t % 2], b * (NT // 2 * 16) + (t // 2 + 1) * 16)
            x = xa[:, t % 2]
            v.inc(e.tensor_copy(l_first[:, t:t + 1], x[:, 0:1]))
            done(e.max(top[:, t], x))
            v.inc(e.tensor_tensor(l_gap[:, t:t + 1], top[:, t, 1:2], top[:, t, 0:1], ALU.subtract))
            e.max_index(top_at[:, t], top[:, t], x).then_inc(xa_read, 1)

        def act_squares(e, b, t):
            e.wait_ge(xa_read, b * NT + t + 1)
            e.activation(xa[:, t % 2], xa[:, t % 2], ACT.Square, accum_out=lead_sq[:, t:t + 1]).then_inc(xa_squared, 1)

        def dve_argmax(e, b, first):
            e.wait_ge(xa_read, b * NT + NT)
            done(e.tensor_copy(argmax_f[:], top_at[:, :, 0]))
            if not first:
                e.wait_ge(argmax_out, b * 16)
                e.wait_ge(index_in, b * (NT * 16))
            done(e.tensor_scalar(argmax_f[:], argmax_f[:], lead_row[:, 0:1], None, ALU.add))
            v.inc(e.tensor_scalar(lead_row[:], lead_row[:], float(N), None, ALU.add))
            e.tensor_copy(argmax[:], argmax_f[:]).then_inc(argmax_made, 1)
            e.wait_ge(v.sem, v.value())

        def dve_leads(e, b):
            e.wait_ge(xa_squared, b * NT + NT)
            e.wait_ge(v.sem, v.value())
            first_max = top[:, :, 0]
            done(e.tensor_scalar(l_var[:], lead_sq[:], 1.0 / D, EPS, ALU.mult, ALU.add))
            rsqrt(e, done, l_var[:], l_rstd[:], l_tmp[:])
            done(e.scalar_tensor_tensor(out=l_gap[:], in0=first_max, scalar=ROUNDINGS, in1=l_gap[:],
                                        op0=ALU.mult, op1=ALU.add))
            done(e.tensor_tensor(l_gap[:], l_gap[:], l_rstd[:], ALU.mult))
            done(e.tensor_reduce(l_far[:], l_gap[:], AX.X, ALU.max))
            done(e.tensor_tensor(lead_max[:], lead_max[:], l_far[:], ALU.max))

        def sp_argmax(e, b):
            e.wait_ge(argmax_made, b + 1)
            with nc.allow_non_contiguous_dma(reason="4 KB of row numbers"):
                e.dma_start(argmax_dram[bass.ds(b * N, N), :].rearrange("(t p) o -> p (t o)", p=P),
                            argmax[:]).then_inc(argmax_out, 16)

        def pool_index(e, b, t):
            e.indirect_dma_start(out=s.index[:, t:t + 1], out_offset=None, in_=argmax_dram,
                                 in_offset=bass.IndirectOffsetOnAxis(ap=argmax[:, t:t + 1], axis=0)
                                 ).then_inc(index_in, 16)

        def dve_bound_weights(e, i):
            part = w0s[0][:, i] if i < KI else w1s[0][:, :, (i - KI) * FO:(i - KI + 1) * FO]
            part = part.bitcast(F32)
            junk = s.products if i < KI else s.products.rearrange("p (c o) -> p c o", c=KD)
            col = Q_W0 + i if i < KI else Q_W1 + i - KI
            done(e.tensor_tensor_reduce(out=junk, in0=part, in1=part, scale=1.0, scalar=0.0, op0=ALU.mult,
                                        op1=ALU.add, accum_out=bounds[:, col:col + 1]))

        def dve_bound_rest(e):
            done(e.tensor_tensor_reduce(out=q[:, 0:H], in0=b0[:], in1=b0[:], scale=1.0, scalar=0.0, op0=ALU.mult,
                                        op1=ALU.add, accum_out=bounds[:, Q_B0:Q_B0 + 1]))
            for i, col in enumerate((Q_A0, Q_A1)):
                done(e.tensor_tensor_reduce(out=att_sq[0:2 * H], in0=att[:, i], in1=att[:, i], scale=1.0, scalar=0.0,
                                            op0=ALU.mult, op1=ALU.add, accum_out=bounds[0:2 * H, col:col + 1]))

        def dve_verdict(e):
            done(e.tensor_copy(bounds[:, Q_CTX:Q_CTX + 1], ctx_max[:]))
            e.tensor_copy(bounds[:, Q_LEAD:Q_LEAD + 1], lead_max[:]).then_inc(bound_made, 1)
            e.wait_ge(bound_spread, 1)
            v.inc(e.reduce_sum(total[:, 0:1], ps[:, 4, 0:P], axis=AX.X))
            done(e.tensor_reduce(total[:, 1:2], ps[:, 4, 0:P], AX.X, ALU.max))
            v.inc(e.tensor_scalar(spread[:, 0], k.ident[:], total[:, 0:1], None, ALU.mult))
            e.tensor_scalar(spread[:, 1], k.ident[:], total[:, 1:2], None, ALU.mult).then_inc(bound_made, 1)
            e.wait_ge(bound_spread, 2)
            done(e.tensor_copy(q[:], ps[:, 4, P:P + 16]))
            sums = ps[:, 4, 0:P]
            root_t, root_y = att_sq[:, 0:1], att_sq[:, 1:2]

            def root(x):
                rsqrt(e, done, x, root_y, root_t)
                done(e.tensor_tensor(x, x, root_y, ALU.mult))
                done(e.tensor_scalar(x, x, 1.01, None, ALU.mult))

            w0, b0n, w1, e0, e1 = (att_sq[:, i:i + 1] for i in range(2, 7))
            done(e.tensor_reduce(w0, sums[:, Q_W0:Q_W0 + KI], AX.X, ALU.add))
            done(e.tensor_copy(b0n, sums[:, Q_B0:Q_B0 + 1]))
            done(e.tensor_reduce(w1, sums[:, Q_W1:Q_W1 + H], AX.X, ALU.max))
            for x in (w0, b0n, w1, q[:, Q_CTX:Q_CTX + 1], q[:, Q_A0:Q_A0 + 1], q[:, Q_A1:Q_A1 + 1]):
                root(x)
            done(e.tensor_tensor(e0, q[:, Q_CTX:Q_CTX + 1], w0, ALU.mult))
            done(e.tensor_tensor(e1, e0, b0n, ALU.add))
            done(e.tensor_tensor(e0, e0, q[:, Q_A0:Q_A0 + 1], ALU.mult))
            done(e.tensor_tensor(e1, e1, w1, ALU.mult))
            done(e.tensor_tensor(e1, e1, q[:, Q_A1:Q_A1 + 1], ALU.mult))
            done(e.tensor_tensor(e0, e0, e1, ALU.add))
            done(e.tensor_scalar(e0, e0, 4.0, UNDERFLOW, ALU.mult, ALU.add))
            done(e.tensor_scalar(q[:, Q_LEAD:Q_LEAD + 1], q[:, Q_LEAD:Q_LEAD + 1], 2.0 * ROUNDINGS, None, ALU.add))
            done(e.scalar_tensor_tensor(out=e1, in0=q[:, Q_LEAD:Q_LEAD + 1], scalar=-MASK, in1=e0,
                                        op0=ALU.mult, op1=ALU.add))
            done(e.tensor_scalar(e1, e1, 0.0, None, ALU.is_lt))
            e.tensor_scalar(flag[:], e1, -1.0, 1.0, ALU.mult, ALU.add).then_inc(bound_made, 1)

        def pe_verdict(e):
            e.wait_ge(bound_made, 1)
            e.matmul(ps[:, 4, 0:P], bounds[:], k.ident[:], start=True, stop=True).then_inc(bound_spread, 1)
            e.wait_ge(bound_made, 2)
            e.matmul(ps[:, 4, 0:P], k.ones[:], spread[:, 0], start=True, stop=True)
            e.matmul(ps[:, 4, P:2 * P], k.ones[:], spread[:, 1], start=True, stop=True).then_inc(bound_spread, 1)

        block = ctx.enter_context(nc.Block())

        @block.sync
        def _(e):
            sp_ctx(e, 0, first=True)
            for c in range(KI):
                e.dma_start(w0_raw[:, c].rearrange("p (h o) -> p h o", h=H), a.w0[:, c]).then_inc(w_in[0], 16)
            with nc.allow_non_contiguous_dma(reason="the bias by partition, 4 KB"):
                e.dma_start(b0[:], a.b0.rearrange("h o -> o h")).then_inc(b0_in, 16)
            for c in range(KD):
                e.dma_start(w1_raw[:, c].rearrange("p (h o) -> p h o", h=H), a.w1[:, c]
                            ).then_inc(w_in[1 + c // (KD // 2)], 16)
                if c == 0:
                    sp_ctx(e, 1)
            e.wait_ge(b1_zero, 1)
            for row in (0, 32):
                e.dma_start(b1_raw[row:row + 1], a.b1).then_inc(b1_in, 16)
            for n in range(2):
                sp_lead(e, n, first=True, par=n)
            for i, src in enumerate((a.as0, a.an0, a.as1, a.an1)):
                e.dma_start(att[i % 2 * H:(i % 2 + 1) * H, i // 2], src).then_inc(att_in, 16)
            s.sp_consts(e)
            sp_ctx(e, 2)

            def graph(b, first=False, last=False):
                for S in range(SLOTS):
                    if S in LEAD_AT and not (last and LEAD_AT[S] + 2 >= NT):
                        sp_lead(e, b * NT + LEAD_AT[S] + 2, par=LEAD_AT[S] % 2)
                    if S in TILE_AT and not first:
                        s.sp_tile(e, b - 1, TILE_AT[S] + 2)
                    if S == 8 and first:
                        e.wait_ge(w0_lo, KI)
                        for t in range(2):
                            s.sp_tile(e, 0, t, first=True)
                    if S % GS == 2 and not (last and S >= GS):
                        sp_ctx(e, b * NQ + S // GS + 3)
                    if S == max(LEAD_AT) + 1:
                        sp_argmax(e, b)
                    if S - 1 in BASE_AT and not first:
                        for t in BASE_AT[S - 1]:
                            s.sp_base(e, b - 1, t)
                    if S % 2:
                        sp_rows(e, b, S // 2)
            over_graphs(e, graph)
            for t in range(2, NT):
                s.sp_tile(e, B - 1, t)
            for t in range(NT):
                s.sp_base(e, B - 1, t)
            f.sp(e)

        @block.gpsimd
        def _(e):
            k.pool(e)

            def graph(b, first=False, last=False):
                for S in range(SLOTS):
                    if S == INDEX_AT:
                        e.wait_ge(argmax_out, (b + 1) * 16)
                        if not first:
                            e.wait_ge(s.diag_made, b * NT)
                    if S == 0 and not first:
                        gathers_ready(b)
                    pool_layer1(e, b, S)
                    if not first:
                        if S < 2:
                            for t in range(S * NT // 2, (S + 1) * NT // 2):
                                s.pool_gather(e, b - 1, t)
                        if 2 <= S < 2 + NT:
                            s.pool_add(e, b - 1, S - 2)
                    if INDEX_AT <= S < INDEX_AT + 2:
                        for t in range((S - INDEX_AT) * NT // 2, (S - INDEX_AT + 1) * NT // 2):
                            pool_index(e, b, t)
                if not first:
                    e.wait_ge(s.base_out, b * (NT * 16))

            def gathers_ready(b):
                for par in y_out:
                    e.wait_ge(par, b * (NT // 2 * 16))
                e.wait_ge(index_in, b * (NT * 16))
                e.wait_ge(w1_lo, KD)
                e.wait_ge(w1_hi, KD)
            over_graphs(e, graph)
            gathers_ready(B)
            for t in range(NT):
                s.pool_gather(e, B - 1, t)
            for t in range(NT):
                s.pool_add(e, B - 1, t)
            f.pool(e)

        @block.vector
        def _(e):
            v.inc(e.memset(bounds[:], 0.0))
            v.inc(e.memset(ctx_max[:], 0.0))
            v.inc(e.memset(lead_max[:], MASK))
            v.inc(e.memset(lead_row[:], 0.0))
            done(e.memset(s.same[:], 0.0))
            e.memset(b1_raw, 0.0).then_inc(b1_zero, 1)
            for row in (0, 32):
                done(e.memset(s.same[row:row + 1], 1.0))
            done(e.tensor_copy(b1_rows[:], s.same[:]))
            k.dve(e)
            dve_turned(e, 0, 0)
            for c in range(KI):
                e.wait_ge(w0_hi, c + 1)
                e.tensor_tensor(w0s[1][:, c], w0_raw[:, c], w0s[0][:, c].bitcast(F32), ALU.subtract).then_inc(w0_lo, 1)
            dve_squares(e, 0)
            for c in range(KD):
                dve_layer0(e, 0, c, 0)
                dve_low0(e, 0, c, 0)
                e.wait_ge(w1_hi, c + 1)
                e.tensor_tensor(w1s[1][:, c], w1_raw[:, c], w1s[0][:, c].bitcast(F32), ALU.subtract).then_inc(w1_lo, 1)
                if c == 3:
                    dve_turned(e, 1, 1)
                    dve_squares(e, 1)
            e.wait_ge(b1_made, 1)
            e.tensor_tensor(b1s[32:33], b1_raw[32:33], b1s[32:33].bitcast(F32), ALU.subtract).then_inc(b1_made, 1)
            e.wait_ge(b1_made, 2)
            s.dve_consts(e)

            def graph(b, first=False, last=False):
                for S in range(SLOTS):
                    if not (last and S >= SLOTS - GS):
                        g, u = b * NQ + S // GS + 1, (S // GS + 1) % 2
                        for c in range(S % GS * 2, S % GS * 2 + 2):
                            dve_layer0(e, g, c, u)
                        for c in range(S % GS * 2, S % GS * 2 + 2):
                            dve_low0(e, g, c, u)
                    if not (last and S >= SLOTS - 2 * GS):
                        if S % GS == 1:
                            dve_squares(e, b * NQ + S // GS + 2)
                        if S % GS == 2:
                            dve_turned(e, b * NQ + S // GS + 2, S // GS % 2)
                    if S in LEAD_AT:
                        dve_lead(e, b, LEAD_AT[S])
                    if S == max(LEAD_AT):
                        dve_argmax(e, b, first)
                    if S == LEADS_AT:
                        dve_leads(e, b)
                    if first:
                        if 3 <= S < 3 + KI + H:
                            dve_bound_weights(e, S - 3)
                        if S == 3 + KI + H:
                            e.wait_ge(att_in, 64)
                            dve_bound_rest(e)
                        dve_layer1(e, b, S)
                        continue
                    if S in TILE_AT:
                        s.dve_tile(e, b - 1, TILE_AT[S])
                    if S == NORM_AT:
                        s.dve_norm(e, b - 1)
                    for t in RANK_AT.get(S, ()):
                        s.dve_rank(e, b - 1, t)
                    if S == max(RANK_AT):
                        s.dve_onehot(e, b - 1)
                    dve_layer1(e, b, S)
                    if S == PICK_AT:
                        s.dve_chosen(e, b - 1)
            graph(0, first=True)
            with e.Fori(1, B - 1) as b:
                v.enter(b, 1, LOOP_STEPS)
                graph(b)
                v.leave(B - 2)
            graph(B - 1, last=True)
            dve_verdict(e)
            for t in range(NT):
                s.dve_tile(e, B - 1, t)
            s.dve_norm(e, B - 1)
            for t in range(NT):
                s.dve_rank(e, B - 1, t)
            s.dve_onehot(e, B - 1)
            s.dve_chosen(e, B - 1)
            f.dve(e)

        @block.scalar
        def _(e):
            act_turned(e, 0, 0)
            e.wait_ge(w_in[0], KI * 16)
            for c in range(KI):
                e.activation(w0s[0][:, c], w0_raw[:, c], ACT.Copy).then_inc(w0_hi, 1)
            e.wait_ge(b0_in, 16)
            for c in range(KD):
                act_layer0(e, 0, c)
                act_high0(e, 0, c, 0)
                e.wait_ge(w_in[1 + c // (KD // 2)], KD // 2 * 16)
                e.activation(w1s[0][:, c], w1_raw[:, c], ACT.Copy).then_inc(w1_hi, 1)
                if c == 3:
                    act_turned(e, 1, 1)
            e.wait_ge(b1_in, 32)
            e.activation(b1s[:], b1_raw, ACT.Copy).then_inc(b1_made, 1)

            def graph(b, first=False, last=False):
                for S in range(SLOTS):
                    if not (last and S >= SLOTS - GS):
                        g, u = b * NQ + S // GS + 1, (S // GS + 1) % 2
                        for c in range(S % GS * 2, S % GS * 2 + 2):
                            act_layer0(e, g, c)
                        for c in range(S % GS * 2, S % GS * 2 + 2):
                            act_high0(e, g, c, u)
                    if S % GS == 2 and not (last and S >= SLOTS - 2 * GS):
                        act_turned(e, b * NQ + S // GS + 2, S // GS % 2)
                    act_layer1(e, b, S)
                    if S in LEAD_AT:
                        act_squares(e, b, LEAD_AT[S])
                    if not first:
                        for t in BASE_AT.get(S, ()):
                            s.act_base(e, b - 1, t)
            over_graphs(e, graph)
            for t in range(NT):
                s.act_base(e, B - 1, t)
            f.act(e)

        @block.tensor
        def _(e):
            k.pe(e)
            pe_turn(e, 0, first=True)
            e.wait_ge(w0_lo, KI)
            for c in range(KD):
                pe_layer0(e, 0, c, 0)
                if c == 2:
                    pe_turn(e, 1)
            e.wait_ge(b1_made, 2)
            e.wait_ge(w1_lo, KD)

            def graph(b, first=False, last=False):
                for S in range(SLOTS):
                    if not (last and S >= SLOTS - GS):
                        for c in range(S % GS * 2, S % GS * 2 + 2):
                            pe_layer0(e, b * NQ + S // GS + 1, c, (S // GS + 1) % 2)
                    pe_layer1(e, b, S)
                    if S % GS == 1 and not (last and S >= SLOTS - 2 * GS):
                        pe_turn(e, b * NQ + S // GS + 2)
                    if not first:
                        if S == NORM_AT:
                            s.pe_spread(e, b - 1)
                        if S == max(RANK_AT):
                            s.pe_pick(e, b - 1)
            over_graphs(e, graph)
            pe_verdict(e)
            s.pe_spread(e, B - 1)
            s.pe_pick(e, B - 1)
            f.pe(e)


def build_full(nc, a, out, rows_dram, flag):
    mask_dram = nc.dram_tensor("mask", (B * N, N), F32, kind="Internal").ap()
    hidden_dram = nc.dram_tensor("hidden", (B * N, D), F32, kind="Internal").ap()
    rows_f32 = nc.dram_tensor("full_rows", (B * N, D), U32, kind="Internal").ap()

    with ExitStack() as ctx:
        def sem(name):
            return ctx.enter_context(nc.semaphore(name + "_full"))

        def maker(stack):
            return lambda name, shape, dt=F32: stack.enter_context(nc.sbuf_tensor(name + "_full", shape, dt))

        def late(stack, name, shape, dt):
            return stack.enter_context(nc.sbuf_tensor(name + "_full", shape, dt))

        ps = ctx.enter_context(nc.psum_tensor("ps_full", [P, 8, HALF], F32))
        small = maker(ctx)
        k = make_constants(small, sem)
        bn, stats = small("m_bn", [P, 2, 6]), small("m_stats", [P, 2])
        var, rstd, tmp = small("m_var", [P, 1]), small("m_rstd", [P, 1]), small("m_tmp", [P, 1])
        own, top, low = small("own", [P, 1]), small("row_max", [P, 1]), small("row_max_neg", [P, 1])
        total, inverse = small("row_sum", [P, 1]), small("row_inv", [P, 1])
        self_all, neigh_all = small("self_all", [P, NT, H]), small("neigh_all", [P, NT, H])
        self_tile, neigh_tile = small("self_tile", [P, H]), small("neigh_tile", [P, H])
        self_head, neigh_head = small("self_head", [P, NT]), small("neigh_head", [P, NT])
        s = make_ending(nc, small, small, late, sem, k, a, out, rows_f32, ps)
        v, done = s.v, s.done
        with ExitStack() as layers:
            big = maker(layers)
            w = big("w", [P, KD, D])
            a_self, a_neigh, bias = big("a_self", [P, D]), big("a_neigh", [P, D]), big("bias", [P, D])
            rows_in = big("rows_in", [P, D])
            rows_T = big("rows_T", [P, KD, P])
            feat = big("feat", [P, NT * D])
            feat_tile, prod = big("feat_tile", [P, D]), big("prod", [P, D])
            feat_head, bias_head = big("feat_head", [P, NT, P]), big("bias_head", [P, P])
            diag = big("diag_n", [P, NT, P])
            mask, score, prob = big("mask_in", [P, N]), big("score", [P, N]), big("prob", [P, N])
            prob_T = big("prob_T", [P, NT, P])
            mixed, below0, res = big("mixed", [P, FO]), big("below0", [P, FO]), big("res", [P, FO])
        f = make_ffn(nc, maker(ctx), sem, k, s, a, out, rows_f32, ps)

        m_in, m_made, m_out, w_in = sem("m_in"), sem("m_made"), sem("m_out"), sem("w_in")
        f_in, f_turned, f_copied, f_made, f_free = (sem("f_" + x) for x in ("in", "turned", "copied", "made", "free"))
        h_diag, h_spread = sem("h_diag"), sem("h_spread")
        t_in, t_scores, t_probs, t_turned, t_copied, t_mixed, t_low, t_exp, t_rows, t_out = (
            sem("t_" + x) for x in ("in", "scores", "probs", "turned", "copied", "mixed", "low", "exp", "rows", "out"))
        index_made = sem("index_made")
        neigh_ps = ps[:, 0:2].rearrange("p a b -> p (a b)")
        turned_ps = ps[:, 2:4].rearrange("p a b -> p (a b)")
        feat_ps = ps[:, 4:6].rearrange("p a b -> p (a b)")
        LAYERS = [
            (KI, a.ctx, a.w0, a.as0, a.an0, a.b0, hidden_dram),
            (KD, hidden_dram, a.w1, a.as1, a.an1, a.b1h, rows_f32.bitcast(F32)),
        ]

        def flat(x):
            return x.rearrange("h o -> (h o)").rearrange("(a d) -> a d", a=1).to_broadcast([P, D])

        def loops(e, L, tile, head, row):
            with e.Fori(0, B) as b:
                if tile:
                    with e.Fori(0, NT) as t:
                        tile(b, t, (L * B * NT + b * NT) + t)
                with e.Fori(0, H) as h:
                    n = (L * B * H + b * H) + h
                    if head:
                        head(b, h, n)
                    with e.Fori(0, NT) as t:
                        row(b, h, t, n * NT + t)

        def whenever_flagged(e, program):
            v_flag = e.value_load(flag[0:1, 0:1])
            with e.If(v_flag > 0):
                program(e)
            e.end_ifs()

        block = ctx.enter_context(nc.Block())

        @block.sync
        def _(e):
            def program(e):
                with e.Fori(0, B * NT) as n:
                    e.dma_start(mask[:], a.x[bass.ds(n * P, P), :]).then_inc(m_in, 16)
                    e.wait_ge(m_made, n + 1)
                    e.dma_start(mask_dram[bass.ds(n * P, P), :], score[:]).then_inc(m_out, 16)
                e.wait_ge(m_out, B * NT * 16)
                for L, (K, src, wsrc, asrc, nsrc, bsrc, dst) in enumerate(LAYERS):
                    for c in range(K):
                        e.dma_start(w[:, c].rearrange("p (h o) -> p h o", h=H), wsrc[:, c]).then_inc(w_in, 16)
                    for to, x in ((a_self, asrc), (a_neigh, nsrc), (bias, bsrc)):
                        e.dma_start(to[:], flat(x)).then_inc(w_in, 16)

                    def tile(b, t, n):
                        e.wait_ge(f_free, n + 1)
                        e.dma_start(rows_in[:, 0:K * P], src[bass.ds((b * NT + t) * P, P), :]).then_inc(f_in, 16)

                    def row(b, h, t, n):
                        e.dma_start(mask[:], mask_dram[bass.ds((b * NT + t) * P, P), :]).then_inc(t_in, 16)
                        e.wait_ge(t_rows, n + 1)
                        e.dma_start(dst[bass.ds((b * NT + t) * P, P), bass.ds(h * FO, FO)], res[:]).then_inc(t_out, 16)
                    loops(e, L, tile, None, row)
                    e.wait_ge(t_out, (L + 1) * B * H * NT * 16)
                s.sp_consts(e)
                for t in range(2):
                    s.sp_tile(e, 0, t, first=True)

                def graph(b, last=False):
                    for t in range(2, NT if last else NT + 2):
                        s.sp_tile(e, b, t)
                    for t in range(NT):
                        s.sp_base(e, b, t)
                with e.Fori(0, B - 1) as b:
                    graph(b)
                graph(B - 1, last=True)
                f.sp(e)
            whenever_flagged(e, program)

        @block.gpsimd
        def _(e):
            def program(e):
                k.pool(e)
                for b in range(B):
                    e.wait_ge(index_made, b + 1)
                    if b:
                        e.wait_ge(s.base_out, b * NT * 16)
                    for t in range(NT):
                        s.pool_gather(e, b, t)
                    for t in range(NT):
                        s.pool_add(e, b, t)
                f.pool(e)
            whenever_flagged(e, program)

        @block.vector
        def _(e):
            def mask_tile(n):
                e.wait_ge(m_in, (n + 1) * 16)
                for h in range(2):
                    done(e.bn_stats(bn[:, h], mask[:, h * HALF:(h + 1) * HALF]))
                v.inc(e.tensor_copy(top[:], mask[:, 0:1]))
                done(e.bn_aggr(stats[:], bn[:].rearrange("p h s -> p (h s)")))
                done(e.tensor_scalar(var[:], stats[:, 1:2], EPS, None, ALU.add))
                rsqrt(e, done, var[:], rstd[:], tmp[:])
                done(e.tensor_scalar(score[:], mask[:], stats[:, 0:1], rstd[:, 0:1], ALU.subtract, ALU.mult))
                done(e.tensor_scalar(score[:], score[:], -1.0, 1.0, ALU.mult, ALU.add))
                e.tensor_scalar(score[:], score[:], MASK, None, ALU.mult).then_inc(m_made, 1)
                e.wait_ge(m_out, (n + 1) * 16)

            def program(e):
                k.dve(e)
                e.memset(top[:], 0.0).then_inc(f_free, 1)
                e.wait_ge(f_free, 1)
                with e.Fori(0, B * NT) as n:
                    v.enter(n, 0, MASK_STEPS)
                    mask_tile(n)
                    v.leave(B * NT)
                weights = 0
                for L, (K, *_) in enumerate(LAYERS):
                    weights += K + 3
                    e.wait_ge(w_in, weights * 16)

                    def tile(b, t, n):
                        e.wait_ge(f_turned, n + 1)
                        e.tensor_copy(rows_T[:, 0:K].rearrange("p c r -> p (c r)"), turned_ps[:, 0:K * P]
                                      ).then_inc(f_copied, 1)
                        e.wait_ge(f_made, n + 1)
                        done(e.tensor_copy(feat_tile[:], feat_ps))
                        v.inc(e.tensor_copy(feat[:, bass.ds(t * D, D)], feat_tile[:]))
                        for att, tile_sum, all_sums in ((a_self, self_tile, self_all), (a_neigh, neigh_tile, neigh_all)):
                            done(e.tensor_tensor(prod[:], feat_tile[:], att[:], ALU.mult))
                            done(e.tensor_reduce(tile_sum[:], prod[:].rearrange("p (h o) -> p h o", h=H), AX.X,
                                                 ALU.add))
                            done(e.tensor_copy(all_sums[:, bass.ds(t, 1)], tile_sum[:]))
                        e.tensor_copy(top[:], feat_tile[:, 0:1]).then_inc(f_free, 1)
                        e.wait_ge(f_free, n + 2)

                    def head(b, h, n):
                        done(e.tensor_copy(self_head[:], self_all[:, :, bass.ds(h, 1)]))
                        done(e.tensor_copy(neigh_head[:], neigh_all[:, :, bass.ds(h, 1)]))
                        done(e.tensor_copy(bias_head[:], bias[:, bass.ds(h * FO, FO)]))
                        done(e.tensor_copy(feat_head[:], feat[:].rearrange("p (t c) -> p t c", t=NT)
                                           [:, :, bass.ds(h * FO, FO)]))
                        for t in range(NT):
                            ins = e.tensor_scalar(diag[:, t], k.ident[:], neigh_head[:, t:t + 1], None, ALU.mult)
                            if t < NT - 1:
                                done(ins)
                        ins.then_inc(h_diag, 1)

                    def row(b, h, t, n):
                        e.wait_ge(h_spread, (L * B * H + b * H) + h + 1)
                        e.wait_ge(t_in, (n + 1) * 16)
                        done(e.tensor_copy(own[:], self_head[:, bass.ds(t, 1)]))
                        done(e.tensor_scalar(score[:], neigh_ps, own[:, 0:1], None, ALU.add))
                        done(e.scalar_tensor_tensor(out=score[:], in0=score[:], scalar=LRELU, in1=score[:],
                                                    op0=ALU.mult, op1=ALU.max))
                        done(e.tensor_tensor(score[:], score[:], mask[:], ALU.add))
                        done(e.tensor_reduce(top[:], score[:], AX.X, ALU.max))
                        e.tensor_scalar(low[:], top[:], -1.0, None, ALU.mult).then_inc(t_scores, 1)
                        e.wait_ge(t_turned, n + 1)
                        e.tensor_copy(prob_T[:].rearrange("p c r -> p (c r)"), turned_ps).then_inc(t_copied, 1)
                        done(e.reciprocal(inverse[:], total[:]))
                        e.wait_ge(t_mixed, n + 1)
                        done(e.scalar_tensor_tensor(out=mixed[:], in0=ps[:, 6, 0:FO], scalar=inverse[:, 0:1],
                                                    in1=bias_head[:], op0=ALU.mult, op1=ALU.add))
                        e.tensor_scalar(below0[:], mixed[:], 0.0, None, ALU.min).then_inc(t_low, 1)
                        done(e.tensor_scalar(mixed[:], mixed[:], 0.0, None, ALU.max))
                        e.wait_ge(t_exp, n + 1)
                        e.scalar_tensor_tensor(out=res[:], in0=below0[:], scalar=-1.0, in1=mixed[:], op0=ALU.add,
                                               op1=ALU.add).then_inc(t_rows, 1)
                        e.wait_ge(t_out, (n + 1) * 16)

                    with e.Fori(0, B) as b:
                        v.enter(b, 0, LAYER_STEPS)
                        with e.Fori(0, NT) as t:
                            v.enter(t, 0, FEAT_STEPS)
                            tile(b, t, (L * B * NT + b * NT) + t)
                            v.leave(NT)
                        with e.Fori(0, H) as h:
                            v.enter(h, 0, HEAD_STEPS + NT * ROW_STEPS)
                            n = (L * B * H + b * H) + h
                            head(b, h, n)
                            assert v.n == HEAD_STEPS, v.n
                            with e.Fori(0, NT) as t:
                                v.enter(t, 0, ROW_STEPS)
                                row(b, h, t, n * NT + t)
                                v.leave(NT)
                            v.leave(H)
                        v.leave(B)
                s.dve_consts(e)

                def graph(b, first=False):
                    if not first:
                        e.wait_ge(index_made, b)
                    e.tensor_copy(s.index[:], s.row[:]).then_inc(index_made, 1)
                    for t in range(NT):
                        s.dve_tile(e, b, t)
                    s.dve_norm(e, b)
                    for t in range(NT):
                        s.dve_rank(e, b, t)
                    s.dve_onehot(e, b)
                    s.dve_chosen(e, b)
                graph(0, first=True)
                with e.Fori(1, B) as b:
                    v.enter(b, 1, END_STEPS)
                    graph(b)
                    v.leave(B - 1)
                f.dve(e)
            whenever_flagged(e, program)

        @block.scalar
        def _(e):
            def program(e):
                def row(b, h, t, n):
                    e.wait_ge(t_scores, n + 1)
                    e.activation(prob[:], score[:], ACT.Exp, bias=low[:, 0:1], accum_out=total[:]).then_inc(t_probs, 1)
                    e.wait_ge(t_low, n + 1)
                    e.activation(below0[:], below0[:], ACT.Exp).then_inc(t_exp, 1)
                for L in range(2):
                    loops(e, L, None, None, row)
                with e.Fori(0, B) as b:
                    for t in range(NT):
                        s.act_base(e, b, t)
                f.act(e)
            whenever_flagged(e, program)

        @block.tensor
        def _(e):
            def program(e):
                k.pe(e)
                weights = 0
                for L, (K, *_) in enumerate(LAYERS):
                    weights += K + 3
                    e.wait_ge(w_in, weights * 16)

                    def tile(b, t, n):
                        e.wait_ge(f_in, (n + 1) * 16)
                        for c in range(K):
                            ins = e.transpose(turned_ps[:, c * P:(c + 1) * P], rows_in[:, c * P:(c + 1) * P], k.ident[:])
                        ins.then_inc(f_turned, 1)
                        e.wait_ge(f_copied, n + 1)
                        for h in range(2):
                            for c in range(K):
                                ins = e.matmul(ps[:, 4 + h], rows_T[:, c], w[:, c, h * HALF:(h + 1) * HALF],
                                               start=(c == 0), stop=(c == K - 1))
                        ins.then_inc(f_made, 1)

                    def head(b, h, n):
                        e.wait_ge(h_diag, n + 1)
                        for t in range(NT):
                            ins = e.matmul(neigh_ps[:, t * P:(t + 1) * P], k.ones[:], diag[:, t], start=True, stop=True)
                        ins.then_inc(h_spread, 1)

                    def row(b, h, t, n):
                        e.wait_ge(t_probs, n + 1)
                        for c in range(NT):
                            ins = e.transpose(turned_ps[:, c * P:(c + 1) * P], prob[:, c * P:(c + 1) * P], k.ident[:])
                        ins.then_inc(t_turned, 1)
                        e.wait_ge(t_copied, n + 1)
                        for c in range(NT):
                            ins = e.matmul(ps[:, 6, 0:FO], prob_T[:, c], feat_head[:, c], start=(c == 0),
                                           stop=(c == NT - 1))
                        ins.then_inc(t_mixed, 1)
                    loops(e, L, tile, head, row)
                with e.Fori(0, B) as b:
                    s.pe_spread(e, b)
                    s.pe_pick(e, b)
                f.pe(e)
            whenever_flagged(e, program)


def build(nc, a, out):
    rows_dram = nc.dram_tensor("layer_rows", (B * N, D), U32, kind="Internal").ap()
    argmax_dram = nc.dram_tensor("argmax_rows", (B * N, 1), U32, kind="Internal").ap()
    with ExitStack() as ctx:
        flag = ctx.enter_context(nc.sbuf_tensor("flag", [P, 1], I32))
        build_lead(nc, a, out, rows_dram, argmax_dram, flag)
        build_full(nc, a, out, rows_dram, flag)


def kernel(**inputs):
    import numpy as _np
    import concourse.bacc as _bacc
    from concourse import mybir as _mybir
    from concourse.bass_utils import run_bass_kernel_spmd as _run

    nc = _bacc.Bacc("TRN2", target_bir_lowering=False, num_devices=1)
    arrays, a = {}, Names()

    def dram(name):
        x = _np.ascontiguousarray(inputs[name])
        arrays[f"in_{name}_dram"] = x
        return nc.dram_tensor(f"in_{name}_dram", x.shape, _mybir.dt.from_np(x.dtype), kind="ExternalInput").ap()

    def by_chunk(w):
        return w.rearrange("h (k p) o -> p k h o", p=P)

    def as_row(w, axes):
        return w.rearrange(f"{axes} -> ({axes})").rearrange("(a d) -> a d", a=1)

    a.x = dram("x").rearrange("b n d -> (b n) d")
    a.ctx = dram("ctx_512").rearrange("b n f -> (b n) f")
    a.w0, a.w1 = by_chunk(dram("L0_xattn_W0")), by_chunk(dram("L0_xattn_W1"))
    a.as0, a.an0, a.b0 = dram("L0_xattn_a_self0"), dram("L0_xattn_a_neigh0"), dram("L0_xattn_b0")
    a.as1, a.an1, a.b1h = dram("L0_xattn_a_self1"), dram("L0_xattn_a_neigh1"), dram("L0_xattn_b1")
    a.b1 = as_row(a.b1h, "h o")
    a.wr, a.br = as_row(dram("L0_ffn_Wr"), "d o"), dram("L0_ffn_br")
    a.fw1, a.fb1 = dram("L0_ffn_W1"), dram("L0_ffn_b1")
    a.fw2, a.fb2 = dram("L0_ffn_W2"), dram("L0_ffn_b2")
    out = nc.dram_tensor("out_0_dram", (B, N, D), F32, kind="ExternalOutput").ap()
    build(nc, a, out.rearrange("b n d -> (b n) d"))
    r = _run(nc, [arrays], core_ids=[0])
    return r.results[0]["out_0_dram"]
```

```python
from contextlib import ExitStack

import concourse.bass as bass
from concourse import mybir

F32 = mybir.dt.float32
F32R = mybir.dt.float32r
I32 = mybir.dt.int32
U32 = mybir.dt.uint32
ALU = mybir.AluOpType
ACT = mybir.ActivationFunctionType
AX = mybir.AxisListType

P = 128
B, N, D = 4, 1024, 1024
FI = 256
H, FO = 8, 128
FF = 4096
TOP = N // 8
NT = N // P
KI = FI // P
KD = D // P
HALF = 512
NV = 5
GROUP = 256
GT = GROUP // P
CAP = N // 2
CT = CAP // P
NQ = CAP // GROUP
SLOTS = 2 * CT
GS = 2 * GT
NF = FF // P
FG = 4
MASK = -1.0e10
LRELU = 0.2
EPS = 1e-5
RSQRT_MAGIC = float(0x5F3759DF)
PARTS = [(0, 0), (0, 1), (1, 0)]
ROUNDINGS = 6.5e-7
UNDERFLOW = 200.0


LOOP_STEPS = 144
MASK_STEPS, FEAT_STEPS, HEAD_STEPS, ROW_STEPS, END_STEPS = 24, 8, 11, 8, 87
LAYER_STEPS = NT * FEAT_STEPS + H * (HEAD_STEPS + NT * ROW_STEPS)


class Names:
    pass


class Count:

    def __init__(self, sem):
        self.sem, self.base, self.n, self.loops = sem, 0, 0, []

    def inc(self, instruction):
        self.n += 1
        return instruction.then_inc(self.sem, 1)

    def value(self):
        return self.base + self.n

    def enter(self, i, first, each):
        self.loops.append((self.base, self.n, each))
        self.base, self.n = (i - first) * each + (self.base + self.n), 0

    def leave(self, turns):
        self.base, n, each = self.loops.pop()
        assert self.n == each, (self.n, each)
        self.n = n + turns * each


def rsqrt(dve, step, v, y, t):
    step(dve.tensor_scalar(y.bitcast(I32), v.bitcast(I32), -0.5, RSQRT_MAGIC, ALU.mult, ALU.add))
    for _ in range(4):
        step(dve.tensor_tensor(t, y, v, ALU.mult))
        step(dve.tensor_tensor(t, t, y, ALU.mult))
        step(dve.tensor_scalar(t, t, -0.5, 1.5, ALU.mult, ALU.add))
        step(dve.tensor_tensor(y, y, t, ALU.mult))


def make_constants(sb, sem):
    k = Names()
    k.ident = sb("ident", [P, P])
    k.ones = sb("ones", [P, P])
    k.below = sb("below", [P, P])
    k.slot_i = sb("slot_i", [P, P], I32)
    k.slot = sb("slot", [P, P])
    k.row_i = sb("row_i", [P, NT], I32)
    k.row = sb("row", [P, NT])
    pool_made, dve_made = sem("pool_made"), sem("dve_made")

    def pool(e):
        e.memset(k.ident[:], 1.0).then_inc(pool_made, 1)
        e.memset(k.ones[:], 1.0).then_inc(pool_made, 1)
        e.memset(k.below[:], 1.0).then_inc(pool_made, 1)
        e.wait_ge(pool_made, 3)
        e.affine_select(out=k.ident[:], in_=k.ident[:], compare_op=ALU.is_equal, fill=0.0, base=0,
                        pattern=[[1, P]], channel_multiplier=-1).then_inc(pool_made, 1)
        e.affine_select(out=k.below[:], in_=k.below[:], compare_op=ALU.is_gt, fill=0.0, base=0,
                        pattern=[[-1, P]], channel_multiplier=1).then_inc(pool_made, 1)
        e.iota(k.slot_i[:], [[1, P]], base=0, channel_multiplier=0).then_inc(pool_made, 1)
        e.iota(k.row_i[:], [[P, NT]], base=0, channel_multiplier=1).then_inc(pool_made, 1)
    k.pool = pool

    def dve(e):
        e.wait_ge(pool_made, 7)
        e.tensor_copy(k.slot[:], k.slot_i[:]).then_inc(dve_made, 1)
        e.tensor_copy(k.row[:], k.row_i[:]).then_inc(dve_made, 1)
        e.wait_ge(dve_made, 2)
    k.dve = dve

    def pe(e):
        e.wait_ge(dve_made, 2)
    k.pe = pe
    return k



def make_ending(nc, sb, big, late, sem, k, a, out, rows_of, ps):
    s = Names()
    s.index = sb("index", [P, NT], U32)
    s.wr_sum = sb("wr_sum", [P, 1])
    s.br = sb("br", [P, 1])
    s.bn = sb("bn", [P, 4, 2, 6])
    s.stats = sb("stats", [P, NT, 2])
    s.dot = sb("dot", [P, NT])
    s.var = sb("var", [P, NT])
    s.rstd = sb("rstd", [P, NT])
    s.tmp = sb("tmp", [P, NT])
    s.scale = sb("scale", [P, NT])
    s.shift = sb("shift", [P, NT])
    s.values = sb("values", [P, NT, NV])
    s.ranks = sb("ranks", [P, NT, 3])
    s.rank = sb("rank", [P, NT])
    s.same = sb("same", [P, P])
    s.chosen = sb("chosen", [P, B * NV])
    s.token = sb("token", [P, B, 2], U32)
    s.weight = sb("weight", [P, B])
    with ExitStack() as place:
        s.w2s = [late(place, "fw2_hi", [P, FG, D], F32R), late(place, "fw2_lo", [P, FG, D], F32R)]
    s.x1 = big("x1", [P, NT, D])
    s.wr = big("wr", [P, D])
    s.diag = big("diag", [P, NT, P])
    s.x1_last = s.x1

    def x1_of(b):
        return s.x1_last if isinstance(b, int) and b == B - 1 else s.x1

    spread_ps = ps[:, 5:7].rearrange("p a b -> p (a b)")
    s.products = spread_ps
    counted = s.diag[:].rearrange("p t c -> p (t c)")
    pick_ps = ps[:, 7, 0:NV]

    s.x_in = [sem("x_in0"), sem("x_in1")]
    s.x1_made = [sem(f"x1_made{t}", True) for t in range(NT)]
    s.base_made = sem("base_made")
    s.base_out = sem("base_out")
    s.consts_in = sem("consts_in")
    s.diag_made = sem("diag_made")
    s.spread = sem("spread")
    s.onehot_made = sem("onehot_made")
    s.picked = sem("picked")
    s.v = Count(sem("dve_step"))

    def done(ins):
        s.v.inc(ins)
        nc.vector.wait_ge(s.v.sem, s.v.value())
    s.done = done

    def sp_consts(e):
        e.dma_start(s.wr[:], a.wr.to_broadcast([P, D])).then_inc(s.consts_in, 16)
        e.dma_start(s.br[:], a.br.rearrange("(a o) -> a o", a=1).to_broadcast([P, 1])).then_inc(s.consts_in, 16)
    s.sp_consts = sp_consts

    def dve_consts(e):
        e.wait_ge(s.consts_in, 32)
        done(e.reduce_sum(s.wr_sum[:], s.wr[:], axis=AX.X))
        done(e.memset(s.ranks[:], 0.0))
    s.dve_consts = dve_consts

    def sp_x(e, b, first=False):
        if not first:
            e.wait_ge(s.base_out, b * (NT * 16))
        for h in range(2):
            e.dma_start(x1_of(b)[:, h * NT // 2:(h + 1) * NT // 2],
                        a.x[bass.ds(b * N + h * (N // 2), N // 2), :].rearrange("(t p) d -> p t d", p=P)
                        ).then_inc(s.x_in[h], 16)
    s.sp_x = sp_x

    def pool_x1(e, b):
        rows, first = rows_of(b)
        for t in range(NT):
            if t % (NT // 2) == 0:
                e.wait_ge(s.x_in[t // (NT // 2)], (b + 1) * 16)
            e.indirect_dma_start(out=x1_of(b)[:, t], out_offset=None, in_=rows, element_offset=first,
                                 in_offset=bass.IndirectOffsetOnAxis(ap=s.index[:, t:t + 1], axis=0),
                                 compute_op=ALU.add).then_inc(s.x1_made[t], 16)
    s.pool_x1 = pool_x1

    def dve_tile(e, b, t):
        before = s.v.value()
        e.wait_ge(s.x1_made[t], (b + 1) * 16)
        for h in range(2):
            s.v.inc(e.bn_stats(s.bn[:, t % 4, h], x1_of(b)[:, t, h * HALF:(h + 1) * HALF]))
        if t:
            e.wait_ge(s.v.sem, before)
        s.v.inc(e.tensor_tensor_reduce(out=s.products, in0=x1_of(b)[:, t], in1=s.wr[:], scale=1.0, scalar=0.0,
                                       op0=ALU.mult, op1=ALU.add, accum_out=s.dot[:, t:t + 1]))
        if t:
            gather_stats(e, t - 1)

    def gather_stats(e, t):
        s.v.inc(e.bn_aggr(s.stats[:, t], s.bn[:, t % 4].rearrange("p h s -> p (h s)")))
    s.dve_tile = dve_tile

    def dve_norm(e, b):
        mean = s.stats[:, :, 0]
        e.wait_ge(s.v.sem, s.v.value())
        s.v.inc(e.tensor_scalar(s.var[:, 0:NT - 1], s.stats[:, 0:NT - 1, 1], EPS, None, ALU.add))
        gather_stats(e, NT - 1)
        e.wait_ge(s.v.sem, s.v.value())
        done(e.tensor_scalar(s.var[:, NT - 1:], s.stats[:, NT - 1:, 1], EPS, None, ALU.add))
        rsqrt(e, done, s.var[:], s.rstd[:], s.tmp[:])
        done(e.tensor_scalar(s.scale[:], s.rstd[:], 1.0, None, ALU.add))
        done(e.tensor_tensor(s.tmp[:], mean, s.rstd[:], ALU.mult))
        done(e.tensor_scalar(s.shift[:], s.tmp[:], -1.0, -1.0, ALU.mult, ALU.add))
        done(e.tensor_scalar(s.tmp[:], mean, s.wr_sum[:, 0:1], -1.0, ALU.mult, ALU.mult))
        done(e.tensor_tensor(s.tmp[:], s.tmp[:], s.dot[:], ALU.add))
        done(e.tensor_tensor(s.tmp[:], s.tmp[:], s.rstd[:], ALU.mult))
        done(e.tensor_scalar(s.values[:, :, 1], s.tmp[:], s.br[:, 0:1], None, ALU.add))
        s.v.inc(e.tensor_copy(s.values[:, :, 0], k.row[:]))
        s.v.inc(e.tensor_copy(s.values[:, :, 2], s.index[:]))
        s.v.inc(e.tensor_copy(s.values[:, :, 3], mean))
        s.v.inc(e.tensor_copy(s.values[:, :, 4], s.rstd[:]))
        e.wait_ge(s.v.sem, s.v.value())
        for t in range(NT):
            e.tensor_scalar(s.diag[:, t], k.ident[:], s.values[:, t, 1:2], None, ALU.mult).then_inc(s.diag_made, 1)
    s.dve_norm = dve_norm

    def act_base(e, b, t):
        e.wait_ge(s.diag_made, b * NT + NT)
        e.activation(x1_of(b)[:, t], x1_of(b)[:, t], ACT.Identity, scale=s.scale[:, t:t + 1],
                     bias=s.shift[:, t:t + 1]).then_inc(s.base_made, 1)
    s.act_base = act_base

    def sp_base(e, b, t):
        e.wait_ge(s.base_made, b * NT + t + 1)
        e.dma_start(out[bass.ds((b * NT + t) * P, P), :], x1_of(b)[:, t]).then_inc(s.base_out, 16)
    s.sp_base = sp_base

    def pe_spread(e, b):
        e.wait_ge(s.diag_made, b * NT + NT)
        for t in range(NT):
            ins = e.matmul(spread_ps[:, t * P:(t + 1) * P], k.ones[:], s.diag[:, t], start=True, stop=True)
        ins.then_inc(s.spread, 1)
    s.pe_spread = pe_spread

    def dve_rank(e, b, t):
        if t == 0:
            e.wait_ge(s.spread, b + 1)
        own, at = s.values[:, t, 1:2], t * P
        last = s.v.value()
        if t:
            e.wait_ge(s.v.sem, s.counted_at)
            s.v.inc(e.tensor_scalar(counted[:, 0:at], spread_ps[:, 0:at], own, 0.0, ALU.is_ge, ALU.add,
                                    accum_out=s.ranks[:, t, 0:1]))
        s.v.inc(e.tensor_scalar(counted[:, at:], spread_ps[:, at:], own, 0.0, ALU.is_gt, ALU.add,
                                accum_out=s.ranks[:, t, 1:2]))
        s.counted_at = s.v.value()
        if t:
            e.wait_ge(s.v.sem, last)
        s.v.inc(e.scalar_tensor_tensor(out=s.same[:], in0=spread_ps[:, at:at + P], scalar=own, in1=k.below[:],
                                       op0=ALU.is_equal, op1=ALU.mult, accum_out=s.ranks[:, t, 2:3]))
    s.dve_rank = dve_rank

    def dve_onehot(e, b):
        e.wait_ge(s.v.sem, s.v.value())
        done(e.reduce_sum(s.rank[:], s.ranks[:], axis=AX.X))
        for t in range(NT):
            e.tensor_scalar(s.diag[:, t], k.slot[:], s.rank[:, t:t + 1], None,
                            ALU.is_equal).then_inc(s.onehot_made, 1)
    s.dve_onehot = dve_onehot

    def pe_pick(e, b):
        e.wait_ge(s.onehot_made, b * NT + NT)
        for t in range(NT):
            ins = e.matmul(pick_ps, s.diag[:, t], s.values[:, t], start=(t == 0), stop=(t == NT - 1))
        ins.then_inc(s.picked, 1)
    s.pe_pick = pe_pick

    def dve_chosen(e, b):
        e.wait_ge(s.picked, b + 1)
        done(e.tensor_copy(s.chosen[:, bass.ds(b * NV, NV)], pick_ps))
    s.dve_chosen = dve_chosen
    return s


def make_ffn(nc, big, sem, k, s, a, out, rows_of, ps):
    f = Names()
    NTOK = B * TOP
    NO = 2 * B
    NGRP = NF // FG
    fx = big("fx", [P, B, D])
    acc = fx
    rows = big("rows", [P, B, D])
    token_fx = big("token_fx", [P, B, 3])
    fxT = [big("fxT_hi", [P, KD, NTOK], F32R), big("fxT_lo", [P, KD, NTOK], F32R)]
    w1 = big("fw1", [P, FG, KD, P])
    w1s = [big("fw1_hi", [P, 2, KD, P], F32R), big("fw1_lo", [P, 2, KD, P], F32R)]
    w2 = big("fw2", [P, FG, D])
    b2 = big("fb2", [P, D])
    w2s = s.w2s
    b1 = big("fb1", [P, NF])
    wl = big("wl", [P, P])
    soft = big("soft", [P, 4])
    hid = big("hid", [P, 2, NTOK])
    hids = [big("hid_hi", [P, FG, NTOK], F32R), big("hid_lo", [P, FG, NTOK], F32R)]
    tok_in = [sem(f"tok_in{b}", True) for b in range(B)]
    fx_made, rows_made, fx_turned = sem("fx_made"), sem("rows_made"), sem("fx_turned")
    fx_hi, fx_lo = sem("fx_hi"), sem("fx_lo")
    w1_in = [sem(f"w1_in{i}") for i in range(FG)]
    w2_in = [sem(f"w2_in{i}") for i in range(FG)]
    w1_hi, w1_lo, w2_hi, w2_lo = sem("w1_hi"), sem("w1_lo"), sem("w2_hi"), sem("w2_lo")
    up_made, gelu, hid_hi, hid_lo = sem("up_made"), sem("gelu"), sem("hid_hi"), sem("hid_lo")
    down_made, added, row_made = sem("down_made"), sem("added"), sem("row_made")
    scattered, bias_in, tok_made = sem("scattered", True), sem("bias_in"), sem("tok_made")
    wl_turned, wl_soft, wl_exp, wl_back = sem("wl_turned"), sem("wl_soft"), sem("wl_exp"), sem("wl_back")
    w1_src = a.fw1.rearrange("(k p) f -> p k f", p=P)
    v, done = s.v, s.done

    def groups(e, turn, first_done=False):
        if not first_done:
            turn(0, True)
        with e.Fori(1, NGRP) as i:
            turn(i, False)

    def sp_biases(e):
        with nc.allow_non_contiguous_dma(reason="the bias by partition, 16 KB"):
            e.dma_start(b1[:], a.fb1.rearrange("(c p) -> p c", p=P)).then_inc(bias_in, 16)
        e.dma_start(b2[:], a.fb2.rearrange("(a d) -> a d", a=1).to_broadcast([P, D])).then_inc(bias_in, 16)

    def sp(e, first):
        def turn(i, first):
            for j in range(FG):
                c = i * FG + j
                if not first:
                    e.wait_ge(w1_hi, c - FG + 1)
                    e.wait_ge(w1_lo, c - FG + 1)
                e.dma_start(w1[:, j], w1_src[:, :, bass.ds(c * P, P)]).then_inc(w1_in[j], 16)
                if not first:
                    e.wait_ge(w2_hi, c - FG + 1)
                    e.wait_ge(w2_lo, c - FG + 1)
                e.dma_start(w2[:, j], a.fw2[bass.ds(c * P, P), :]).then_inc(w2_in[j], 16)
                if first and j == 0:
                    sp_biases(e)
        if first:
            turn(0, True)
        else:
            groups(e, turn, first_done=True)
    f.sp = sp

    def pool_tokens(e, b):
        rows_source, first = rows_of(b)
        e.wait_ge(tok_made, b + 1)
        e.indirect_dma_start(out=rows[:, b], out_offset=None, in_=a.x, element_offset=b * N * D,
                             in_offset=bass.IndirectOffsetOnAxis(ap=s.token[:, b, 0:1], axis=0)
                             ).then_inc(tok_in[b], 16)
        e.wait_ge(tok_in[b], 16)
        e.indirect_dma_start(out=rows[:, b], out_offset=None, in_=rows_source, element_offset=first,
                             in_offset=bass.IndirectOffsetOnAxis(ap=s.token[:, b, 1:2], axis=0),
                             compute_op=ALU.add).then_inc(tok_in[b], 16)
    f.pool_tokens = pool_tokens

    def pool(e):
        e.wait_ge(s.base_out, B * NT * 16)
        for b in range(B):
            e.wait_ge(row_made, b + 1)
            e.indirect_dma_start(out=out, element_offset=b * N * D,
                                 out_offset=bass.IndirectOffsetOnAxis(ap=s.token[:, b, 0:1], axis=0),
                                 in_=rows[:, b], in_offset=None).then_inc(scattered, 16)
        e.wait_ge(scattered, B * 16)
    f.pool = pool

    def dve_tokens(e, b):
        at = b * NV
        mean, rstd = s.chosen[:, at + 3:at + 4], s.chosen[:, at + 4:at + 5]
        if b == 0:
            done(e.memset(wl[:], 0.0))
        v.inc(e.tensor_copy(s.token[:, b, 0:1], s.chosen[:, at:at + 1]))
        v.inc(e.tensor_copy(s.token[:, b, 1:2], s.chosen[:, at + 2:at + 3]))
        v.inc(e.tensor_scalar(token_fx[:, b, 1:2], rstd, 1.0, None, ALU.add))
        done(e.tensor_scalar(token_fx[:, b, 0:1], mean, rstd, -1.0, ALU.mult, ALU.mult))
        done(e.tensor_scalar(token_fx[:, b, 2:3], token_fx[:, b, 0:1], -1.0, None, ALU.add))
        e.tensor_copy(wl[:, b:b + 1], s.chosen[:, at + 1:at + 2]).then_inc(tok_made, 1)
    f.dve_tokens = dve_tokens

    def act_rows(e, b):
        e.wait_ge(tok_in[b], 32)
        e.wait_ge(tok_made, b + 1)
        e.activation(fx[:, b], rows[:, b], ACT.Identity, scale=s.chosen[:, b * NV + 4:b * NV + 5],
                     bias=token_fx[:, b, 0:1]).then_inc(fx_made, 1)
        e.wait_ge(fx_made, b + 1)
        e.activation(rows[:, b], rows[:, b], ACT.Identity, scale=token_fx[:, b, 1:2],
                     bias=token_fx[:, b, 2:3]).then_inc(rows_made, 1)
    f.act_rows = act_rows

    def pe_turned(e, b):
        e.wait_ge(fx_made, b + 1)
        for q in (2 * b, 2 * b + 1):
            c0 = q % 2 * 4
            if q >= 4:
                e.wait_ge(fx_lo, q - 3)
            for c in range(4):
                ins = e.transpose(ps[:, q % 4, c * P:(c + 1) * P], fx[:, b, (c0 + c) * P:(c0 + c + 1) * P], k.ident[:])
            ins.then_inc(fx_turned, 1)
    f.pe_turned = pe_turned

    def act_turned(e, b):
        for q in (2 * b, 2 * b + 1):
            c = q % 2 * 4
            e.wait_ge(fx_turned, q + 1)
            e.activation(fxT[0][:, c:c + 4, b * P:(b + 1) * P], ps[:, q % 4].rearrange("p (c j) -> p c j", c=4),
                         ACT.Copy).then_inc(fx_hi, 1)
    f.act_turned = act_turned

    def dve_turned(e, b):
        for q in (2 * b, 2 * b + 1):
            c = q % 2 * 4
            e.wait_ge(fx_hi, q + 1)
            e.tensor_tensor(fxT[1][:, c:c + 4, b * P:(b + 1) * P], ps[:, q % 4].rearrange("p (c j) -> p c j", c=4),
                            fxT[0][:, c:c + 4, b * P:(b + 1) * P].bitcast(F32), ALU.subtract).then_inc(fx_lo, 1)
    f.dve_turned = dve_turned

    def w1_low(e, c, j, first):
        e.wait_ge(w1_hi, c + 1)
        if not first:
            e.wait_ge(up_made, c - 1)
        e.tensor_tensor(w1s[1][:, j % 2], w1[:, j], w1s[0][:, j % 2].bitcast(F32), ALU.subtract).then_inc(w1_lo, 1)

    def dve_weights(e):
        w1_low(e, 0, 0, True)
        w1_low(e, 1, 1, True)
    f.dve_weights = dve_weights

    def dve(e, beside=None):
        e.wait_ge(wl_turned, 1)
        done(e.tensor_reduce(soft[:, 0:1], ps[:, 4, 0:P], AX.X, ALU.max))
        e.tensor_scalar(soft[:, 1:2], soft[:, 0:1], -1.0, None, ALU.mult).then_inc(wl_soft, 1)
        e.wait_ge(wl_exp, 1)
        done(e.reciprocal(soft[:, 3:4], soft[:, 2:3]))
        e.tensor_scalar(wl[:], wl[:], soft[:, 3:4], None, ALU.mult).then_inc(wl_soft, 1)
        e.wait_ge(wl_back, 1)
        done(e.tensor_copy(s.weight[:], ps[:, 4, 0:B]))
        e.wait_ge(bias_in, 32)
        e.wait_ge(fx_turned, NO)
        for b in range(B):
            v.inc(e.tensor_copy(acc[:, b], b2[:]))
        e.wait_ge(v.sem, v.value())

        def w2_low(c, j, i, first):
            e.wait_ge(w2_hi, c + 1)
            if not first:
                e.wait_ge(down_made, i * NO)
            e.tensor_tensor(w2s[1][:, j], w2[:, j], w2s[0][:, j].bitcast(F32), ALU.subtract).then_inc(w2_lo, 1)

        def turn(i, first=False, last=False):
            for j in range(FG):
                c = i * FG + j
                w2_low(c, j, i, first)
                if j < FG - 2:
                    w1_low(e, c + 2, j + 2, False)
                e.wait_ge(hid_hi, c + 1)
                if not first:
                    e.wait_ge(down_made, i * NO)
                e.tensor_tensor(hids[1][:, j], hid[:, j % 2], hids[0][:, j].bitcast(F32),
                                ALU.subtract).then_inc(hid_lo, 1)
            if not last:
                for j in range(2):
                    w1_low(e, (i + 1) * FG + j, j, False)
            for o in range(NO):
                b, h = o // 2, o % 2
                e.wait_ge(down_made, i * NO + o + 1)
                if not first:
                    e.wait_ge(added, (i - 1) * NO + o + 1)
                e.tensor_tensor(acc[:, b, h * HALF:(h + 1) * HALF], acc[:, b, h * HALF:(h + 1) * HALF],
                                ps[:, 2 + o % 2], ALU.add).then_inc(added, 1)
                if last and h:
                    e.wait_ge(added, i * NO + o + 1)
                    if b == 0:
                        e.wait_ge(rows_made, B)
                    e.scalar_tensor_tensor(out=rows[:, b], in0=acc[:, b], scalar=s.weight[:, b:b + 1],
                                           in1=rows[:, b], op0=ALU.mult, op1=ALU.add).then_inc(row_made, 1)

        turn(0, first=True)
        if beside:
            beside(e)
        with e.Fori(1, NGRP - 1) as i:
            turn(i)
        turn(NGRP - 1, last=True)
    f.dve = dve

    def w1_high(e, i, j, first=False):
        e.wait_ge(w1_in[j], (i + 1) * 16)
        if not first:
            e.wait_ge(up_made, i * FG + j - 1)
        e.activation(w1s[0][:, j % 2], w1[:, j], ACT.Copy).then_inc(w1_hi, 1)

    def act_weights(e):
        w1_high(e, 0, 0, first=True)
        w1_high(e, 0, 1, first=True)
    f.act_weights = act_weights

    def act(e):
        e.wait_ge(wl_soft, 1)
        e.activation(wl[:], ps[:, 4, 0:P], ACT.Exp, bias=soft[:, 1:2], accum_out=soft[:, 2:3]).then_inc(wl_exp, 1)
        e.wait_ge(bias_in, 32)
        e.wait_ge(s.base_out, B * NT * 16)

        def turn(i, first=False, last=False):
            for j in range(FG):
                c = i * FG + j
                e.wait_ge(w2_in[j], (i + 1) * 16)
                if not first:
                    e.wait_ge(down_made, i * NO)
                e.activation(w2s[0][:, j], w2[:, j], ACT.Copy).then_inc(w2_hi, 1)
                if j < FG - 2:
                    w1_high(e, i, j + 2)
                e.wait_ge(up_made, c + 1)
                if not (first and j < 2):
                    e.wait_ge(hid_lo, c - 1)
                e.activation(hid[:, j % 2], ps[:, j % 2], ACT.Gelu, bias=b1c(i, j)).then_inc(gelu, 1)
                e.wait_ge(gelu, c + 1)
                e.activation(hids[0][:, j], hid[:, j % 2], ACT.Copy).then_inc(hid_hi, 1)
            if not last:
                for j in range(2):
                    w1_high(e, i + 1, j)

        def b1c(i, j):
            return b1[:, i * FG + j:i * FG + j + 1] if isinstance(i, int) else b1[:, bass.ds(i * FG + j, 1)]

        turn(0, first=True)
        with e.Fori(1, NGRP - 1) as i:
            turn(i)
        turn(NGRP - 1, last=True)
    f.act = act

    def pe(e):
        e.wait_ge(tok_made, B)
        e.matmul(ps[:, 4, 0:P], wl[:], k.ident[:], start=True, stop=True).then_inc(wl_turned, 1)
        e.wait_ge(wl_soft, 2)
        e.matmul(ps[:, 4, 0:B], wl[:], k.ident[:, 0:B], start=True, stop=True).then_inc(wl_back, 1)
        e.wait_ge(fx_lo, NO)

        def turn(i, first):
            for j in range(FG):
                c = i * FG + j
                e.wait_ge(w1_lo, c + 1)
                if not (first and j < 2):
                    e.wait_ge(gelu, c - 1)
                for kk in range(KD):
                    for n, (w, x) in enumerate(PARTS):
                        ins = e.matmul(ps[:, j % 2], w1s[w][:, j % 2, kk], fxT[x][:, kk],
                                       start=(kk == 0 and n == 0), stop=(kk == KD - 1 and n == 2))
                ins.then_inc(up_made, 1)
            for o in range(NO):
                b, h = o // 2, o % 2
                if not (first and o < 2):
                    e.wait_ge(added, i * NO + o - 1)
                for j in range(FG):
                    if o == 0:
                        e.wait_ge(w2_lo, i * FG + j + 1)
                        e.wait_ge(hid_lo, i * FG + j + 1)
                    for n, (w, x) in enumerate(PARTS):
                        ins = e.matmul(ps[:, 2 + o % 2], hids[w][:, j, b * P:(b + 1) * P],
                                       w2s[x][:, j, h * HALF:(h + 1) * HALF],
                                       start=(j == 0 and n == 0), stop=(j == FG - 1 and n == 2))
                ins.then_inc(down_made, 1)
        groups(e, turn)
    f.pe = pe
    return f


def build_lead(nc, kept, a, out, rows_dram, argmax_dram, place_dram, flag):
    LOAD_AT = {0: range(0, 4), 1: (4, 5), 2: (6, 7)}
    LEAD_AT = {S: (2 * S, 2 * S + 1) for S in range(NT // 2)}
    CHUNKS_G1 = {1: range(0, 3), 2: range(3, 6), 3: range(6, KD)}
    CHUNKS_NEXT_G0 = {6: range(KD)}
    ARGMAX_AT, LEADS_AT, ROWS_AT = 3, 4, 5
    TILE_AT = {4: range(0, 3), 5: range(3, NT)}
    TILE_AT_LAST = {1 + i: (2 * i, 2 * i + 1) for i in range(NT // 2)}
    SQUARE_AT = {SLOTS - NT // 2 + i: i for i in range(NT // 2)}
    NORM_AT, RANK_AT = 6, 7
    BASE_AT = {6: range(0, 4), 7: range(4, NT)}
    Q_W0, Q_B0, Q_W1, Q_CTX, Q_A, Q_LEAD = 0, 2, 3, 11, 12, 13

    with ExitStack() as ctx:
        sems = []

        def sem(name, indirect=False):
            if indirect:
                return kept.enter_context(nc.semaphore(name))
            sems.append(ctx.enter_context(nc.semaphore(name)))
            return sems[-1]

        def maker(stack):
            return lambda name, shape, dt=F32: stack.enter_context(nc.sbuf_tensor(name, shape, dt))

        def late(stack, name, shape, dt):
            return stack.enter_context(nc.sbuf_tensor(name, shape, dt))

        ps = ctx.enter_context(nc.psum_tensor("ps", [P, 8, HALF], F32))
        small = maker(ctx)
        k = make_constants(small, sem)
        b0 = small("b0", [P, H])
        att = small("att", [4 * H, FO])
        scratch = small("scratch", [P, 20])
        bounds = small("bounds", [P, P])
        total = small("total", [P, 2])
        q = small("q", [P, 16])
        lead_sq = small("lead_sq", [P, NT])
        top = small("top", [P, NT, 8])
        top_at = small("top_at", [P, NT, 8], U32)
        argmax = small("argmax", [P, NT], U32)
        twice = small("twice", [P, NT], U32)
        bits = small("bits", [P, 2, NT], U32)
        parts = small("parts", [P, 2, NT])
        upper = small("upper", [P, NT, NT])
        present = small("present", [P, NT + 1])
        place = small("place", [P, NT + 1])
        place_i = small("place_i", [P, NT], U32)
        place_f = small("place_f", [P, NT])
        place_out = small("place_out", [P, NT], U32)
        wanted = small("wanted", [P, NT])
        listed_rows = small("listed_rows", [P, NT, CT])
        most = small("most", [P, 1])
        ctx_list = small("ctx_list", [P, CT], U32)
        next_index = small("next_index", [P, NT], U32)
        l_var, l_rstd, l_tmp = small("l_var", [P, NT]), small("l_rstd", [P, NT]), small("l_tmp", [P, NT])
        l_gap, l_far, l_first = small("l_gap", [P, NT]), small("l_far", [P, 1]), small("l_first", [P, NT])
        ctx_sq = small("ctx_sq", [P, B * NT // 2])
        lead_max = small("lead_max", [P, 1])

        
        def rows_of(b):
            return rows_dram[b], 0

        s = make_ending(nc, small, small, late, sem, k, a, out, rows_of, ps)
        v, done = s.v, s.done
        spread = s.diag
        with ExitStack() as layers:
            big = maker(layers)
            w1s = [big("w1_hi", [P, KD, D], F32R), big("w1_lo", [P, KD, D], F32R)]
            b1s = big("b1s", [P, D], F32R)
            b1_rows = big("b1_rows", [P, P], F32R)
            cx = big("cx", [P, CT, FI])
            cs = big("cs", [P, 2 * FI])
            cxT = [big("cxT_hi", [P, KI, GROUP], F32R), big("cxT_lo", [P, KI, GROUP], F32R)]
            hT = [big("hT_hi", [P, 2, KD, GROUP], F32R), big("hT_lo", [P, 2, KD, GROUP], F32R)]
            relu0, exp0 = big("relu0", [P, 2, GROUP]), big("exp0", [P, 4, GROUP])
            relu1 = big("relu1", [P, 2, HALF])
            y = big("y", [P, 2, D])
            with ExitStack() as shared:
                s.x1_last = late(shared, "x1_last", [P, NT, D], F32)
            w0s = [big("w0_hi", [P, KI, D], F32R), big("w0_lo", [P, KI, D], F32R)]
            xa = big("xa", [P, 4, D])
        ffn_ctx = ctx.enter_context(ExitStack())
        f = make_ffn(nc, maker(ffn_ctx), sem, k, s, a, out, rows_of, ps)
        w0_raw, w1_raw = y, s.x1
        b1_raw = s.diag[:].rearrange("p t c -> p (t c)")
        count_ps, place_ps, list_ps = ps[:, 7, 16:16 + NT], ps[:, 7, 32:33 + NT], ps[:, 7, 48:48 + CT]

        w_in = [sem("w0_in"), sem("w1_in_a"), sem("w1_in_b")]
        w0_hi, w0_lo, w1_hi, w1_lo = sem("lw0_hi"), sem("lw0_lo"), sem("lw1_hi"), sem("lw1_lo")
        b0_in, b1_in, b1_zero, b1_made = sem("b0_in"), sem("b1_in"), sem("b1_zero"), sem("b1_made")
        att_in = sem("att_in")
        cx_in, cx_turned, cx_hi, cx_lo = sem("cx_in", True), sem("cx_turned"), sem("cx_hi"), sem("cx_lo")
        cs_in, cs_squared = sem("cs_in"), sem("cs_squared")
        pairs_made, pairs_counted, present_made = sem("pairs_made"), sem("pairs_counted"), sem("present_made")
        placed, table_made, table_out, list_ready = sem("placed"), sem("table_made"), sem("table_out"), sem("list_ready")
        listed, list_made, index_moved = sem("listed"), sem("list_made"), sem("index_moved")
        slot_in = sem("slot_in", True)
        l0_made, l0_acts, h_sum, h_high, h_lo = (sem(x) for x in ("l0_made", "l0_acts", "h_sum", "h_high", "h_lo"))
        l1_made, l1_acts, y_made = sem("l1_made"), sem("l1_acts"), sem("y_made")
        y_out = [sem("y_out0"), sem("y_out1")]
        xa_in = [sem(f"xa_in{i}") for i in range(4)]
        xa_read, xa_squared, argmax_made, argmax_out = sem("xa_read"), sem("xa_squared"), sem("argmax_made"), sem("argmax_out")
        index_in, bound_made, bound_spread = sem("index_in", True), sem("bound_made"), sem("bound_spread_made")


        def over_graphs(e, body):
            body(0, first=True)
            with e.Fori(1, B - 1) as b:
                body(b)
            body(B - 1, last=True)

        def pe_turn(e, b, gq, first=False):
            g = b * NQ + gq
            e.wait_ge(cx_in, (b + 1) * (CT * 16))
            if not first:
                e.wait_ge(cx_lo, g)
            for r in range(GT):
                for c in range(KI):
                    ins = e.transpose(ps[:, 4, (c * GT + r) * P:(c * GT + r + 1) * P],
                                      cx[:, gq * GT + r, c * P:(c + 1) * P], k.ident[:])
            ins.then_inc(cx_turned, 1)

        def act_turned(e, g, first=False):
            e.wait_ge(cx_turned, g + 1)
            if not first:
                e.wait_ge(l0_made, g * KD)
            e.activation(cxT[0][:], ps[:, 4].rearrange("p (c r) -> p c r", c=KI), ACT.Copy).then_inc(cx_hi, 1)

        def dve_turned(e, g):
            e.wait_ge(cx_hi, g + 1)
            e.tensor_tensor(cxT[1][:], ps[:, 4].rearrange("p (c r) -> p c r", c=KI),
                            cxT[0][:].bitcast(F32), ALU.subtract).then_inc(cx_lo, 1)

        def sp_square(e, n, first=False):
            if not first:
                e.wait_ge(cs_squared, n)
            e.dma_start(cs[:].rearrange("p (r f) -> p r f", r=2),
                        a.ctx[bass.ds(n * (2 * P), 2 * P), :].rearrange("(r p) f -> p r f", p=P)).then_inc(cs_in, 16)

        def act_square(e, n):
            e.wait_ge(cs_in, (n + 1) * 16)
            column = ctx_sq[:, n:n + 1] if isinstance(n, int) else ctx_sq[:, bass.ds(n, 1)]
            e.activation(cs[:], cs[:], ACT.Square, accum_out=column).then_inc(cs_squared, 1)

        def pe_layer0(e, g, c):
            n = g * KD + c
            if c == 0:
                e.wait_ge(cx_lo, g + 1)
            if not (isinstance(n, int) and n < 2):
                e.wait_ge(l0_acts, 2 * (n - 1))
            for kk in range(KI):
                for i, (w, x) in enumerate(PARTS):
                    ins = e.matmul(ps[:, c % 2, 0:GROUP], w0s[w][:, kk, c * P:(c + 1) * P], cxT[x][:, kk],
                                   start=(kk == 0 and i == 0), stop=(kk == KI - 1 and i == 2))
            ins.then_inc(l0_made, 1)

        def act_layer0(e, g, c):
            n = g * KD + c
            e.wait_ge(l0_made, n + 1)
            if not (isinstance(n, int) and n < 2):
                e.wait_ge(h_sum, n - 1)
            if not (isinstance(n, int) and n < 4):
                e.wait_ge(h_lo, n - 3)
            z = ps[:, c % 2, 0:GROUP]
            e.activation(relu0[:, c % 2], z, ACT.Relu, bias=b0[:, c:c + 1]).then_inc(l0_acts, 1)
            e.activation(exp0[:, c % 4], z, ACT.Exp, bias=b0[:, c:c + 1]).then_inc(l0_acts, 1)

        def dve_layer0(e, g, c, u):
            n = g * KD + c
            e.wait_ge(l0_acts, 2 * (n + 1))
            e.scalar_tensor_tensor(out=exp0[:, c % 4], in0=exp0[:, c % 4], scalar=1.0, in1=relu0[:, c % 2],
                                   op0=ALU.min, op1=ALU.add).then_inc(h_sum, 1)

        def act_high0(e, g, c, u):
            e.wait_ge(h_sum, g * KD + c + 1)
            if not (isinstance(g, int) and g < 2):
                e.wait_ge(l1_made, (g - 1) * GS)
            e.activation(hT[0][:, u, c], exp0[:, c % 4], ACT.Copy, bias=-1.0).then_inc(h_high, 1)

        def dve_low0(e, g, c, u):
            e.wait_ge(h_high, g * KD + c + 1)
            e.scalar_tensor_tensor(out=hT[1][:, u, c], in0=exp0[:, c % 4], scalar=-1.0,
                                   in1=hT[0][:, u, c].bitcast(F32), op0=ALU.add,
                                   op1=ALU.subtract).then_inc(h_lo, 1)

        def pe_layer1(e, b, S):
            g, r, h, u = b * NQ + S // GS, S // 2 % GT, S % 2, S // GS % 2
            n = b * SLOTS + S
            if S % GS == 0:
                e.wait_ge(h_lo, (g + 1) * KD)
            if not (isinstance(n, int) and n < 2):
                e.wait_ge(l1_acts, 2 * (n - 1))
            z = ps[:, 2 + h]
            cols = slice(h * HALF, (h + 1) * HALF)
            e.matmul(z, b1_rows[:], b1s[:, cols], start=True, stop=False)
            for kk in range(KD):
                for i, (w, x) in enumerate(PARTS):
                    ins = e.matmul(z, hT[w][:, u, kk, r * P:(r + 1) * P], w1s[x][:, kk, cols], start=False,
                                   stop=(kk == KD - 1 and i == 2))
            ins.then_inc(l1_made, 1)

        def act_layer1(e, b, S):
            n, h, r = b * SLOTS + S, S % 2, S // 2
            e.wait_ge(l1_made, n + 1)
            if not (isinstance(n, int) and n < 2):
                e.wait_ge(y_made, n - 1)
            e.activation(relu1[:, h], ps[:, 2 + h], ACT.Relu).then_inc(l1_acts, 1)
            if not (isinstance(b, int) and b * CT + r < 2):
                e.wait_ge(y_out[r % 2], b * (CT // 2 * 16) + r // 2 * 16)
            e.activation(y[:, r % 2, h * HALF:(h + 1) * HALF], ps[:, 2 + h], ACT.Exp).then_inc(l1_acts, 1)

        def dve_layer1(e, b, S):
            n, h, r = b * SLOTS + S, S % 2, S // 2
            e.wait_ge(l1_acts, 2 * (n + 1))
            yh = y[:, r % 2, h * HALF:(h + 1) * HALF]
            e.scalar_tensor_tensor(out=yh, in0=yh, scalar=1.0, in1=relu1[:, h], op0=ALU.min,
                                   op1=ALU.add).then_inc(y_made, 1)

        def sp_rows(e, b, r):
            e.wait_ge(y_made, b * SLOTS + 2 * r + 2)
            e.dma_start(rows_dram[b][r * P:(r + 1) * P, :], y[:, r % 2]).then_inc(y_out[r % 2], 16)

        def sp_lead(e, n, first=False, par=0):
            if not first:
                e.wait_ge(xa_squared, n - 3)
                e.wait_ge(xa_read, n - 3)
            e.dma_start(xa[:, par], a.x[bass.ds(n * P, P), :]).then_inc(xa_in[par], 16)

        def dve_lead(e, b, t):
            e.wait_ge(xa_in[t % 4], b * (NT // 4 * 16) + (t // 4 + 1) * 16)
            x = xa[:, t % 4]
            v.inc(e.tensor_copy(l_first[:, t:t + 1], x[:, 0:1]))
            done(e.max(top[:, t], x))
            v.inc(e.tensor_tensor(l_gap[:, t:t + 1], top[:, t, 1:2], top[:, t, 0:1], ALU.subtract))
            e.max_index(top_at[:, t], top[:, t], x).then_inc(xa_read, 1)

        def act_squares(e, b, t):
            e.wait_ge(xa_in[t % 4], b * (NT // 4 * 16) + (t // 4 + 1) * 16)
            if not (isinstance(b, int) and b + t == 0):
                e.wait_ge(xa_squared, b * NT + t)
            e.activation(s.products, xa[:, t % 4], ACT.Square, accum_out=lead_sq[:, t:t + 1]).then_inc(xa_squared, 1)

        def dve_argmax(e, b, first=False):
            e.wait_ge(xa_read, b * NT + NT)
            if not first:
                e.wait_ge(argmax_out, b * 16)
                e.wait_ge(index_in, b * (NT * 16))
            e.tensor_copy(argmax[:], top_at[:, :, 0]).then_inc(argmax_made, 1)

        def dve_leads(e, b):
            e.wait_ge(xa_squared, b * NT + NT)
            e.wait_ge(v.sem, v.value())
            first_max = top[:, :, 0]
            done(e.tensor_scalar(l_var[:], lead_sq[:], 1.0 / D, EPS, ALU.mult, ALU.add))
            rsqrt(e, done, l_var[:], l_rstd[:], l_tmp[:])
            done(e.scalar_tensor_tensor(out=l_gap[:], in0=first_max, scalar=ROUNDINGS, in1=l_gap[:],
                                        op0=ALU.mult, op1=ALU.add))
            done(e.tensor_tensor(l_gap[:], l_gap[:], l_rstd[:], ALU.mult))
            done(e.tensor_reduce(l_far[:], l_gap[:], AX.X, ALU.max))
            done(e.tensor_tensor(lead_max[:], lead_max[:], l_far[:], ALU.max))

        def sp_argmax(e, b):
            e.wait_ge(argmax_made, b + 1)
            with nc.allow_non_contiguous_dma(reason="4 KB of row numbers"):
                e.dma_start(argmax_dram[b].rearrange("(t p) o -> p (t o)", p=P),
                            argmax[:]).then_inc(argmax_out, 16)

        def pool_twice(e, b):
            e.wait_ge(argmax_out, (b + 1) * 16)
            if b:
                e.wait_ge(slot_in, b * (NT * 16))
            for t in range(NT):
                e.indirect_dma_start(out=twice[:, t:t + 1], out_offset=None, in_=argmax_dram[b],
                                     in_offset=bass.IndirectOffsetOnAxis(ap=argmax[:, t:t + 1], axis=0)
                                     ).then_inc(index_in, 16)

        def split_7(e, x, to):
            v.inc(e.tensor_scalar(bits[:, 0], x, P - 1, None, ALU.bitwise_and))
            done(e.tensor_scalar(bits[:, 1], x, 7, None, ALU.logical_shift_right))
            done(e.tensor_copy(to, bits[:]))

        def dve_pairs(e, b, first=False):
            e.wait_ge(index_in, (b + 1) * (NT * 16))
            split_7(e, twice[:], parts[:])
            for t in range(NT):
                e.tensor_scalar(s.diag[:, t], k.slot[:], parts[:, 0, t:t + 1], None, ALU.is_equal).then_inc(pairs_made, 1)
                e.tensor_scalar(upper[:, t], k.slot[:, 0:NT], parts[:, 1, t:t + 1], None,
                                ALU.is_equal).then_inc(pairs_made, 1)

        def pe_count(e, b):
            e.wait_ge(pairs_made, (b + 1) * (2 * NT))
            for t in range(NT):
                ins = e.matmul(count_ps, s.diag[:, t], upper[:, t], start=(t == 0), stop=(t == NT - 1))
            ins.then_inc(pairs_counted, 1)

        def dve_present(e, b):
            e.wait_ge(pairs_counted, b + 1)
            e.tensor_scalar(present[:, 0:NT], count_ps, 1.0, None, ALU.min).then_inc(present_made, 1)

        def pe_place(e, b):
            e.wait_ge(present_made, b + 1)
            e.matmul(place_ps, k.below[:], present[:], start=True, stop=False)
            for t in range(NT):
                ins = e.matmul(place_ps[:, t + 1:], k.ones[:], present[:, t:t + 1].to_broadcast([P, NT - t]),
                               start=False, stop=(t == NT - 1))
            ins.then_inc(placed, 1)

        def dve_place(e, b, first=False):
            e.wait_ge(placed, b + 1)
            if not first:
                e.wait_ge(table_out, b * 16)
            done(e.tensor_copy(place[:], place_ps))
            v.inc(e.tensor_tensor(wanted[:], k.row[:], present[:, 0:NT], ALU.mult))
            v.inc(e.tensor_tensor(most[:], most[:], place[:, NT:NT + 1], ALU.max))
            v.inc(e.tensor_scalar(place_f[:], place[:, 0:NT], float(CAP - 1), None, ALU.min))
            done(e.tensor_copy(place_i[:], place[:, 0:NT]))
            split_7(e, place_i[:], parts[:])
            for t in range(NT):
                e.tensor_scalar(s.diag[:, t], k.slot[:], parts[:, 0, t:t + 1], None, ALU.is_equal).then_inc(list_ready, 1)
                e.tensor_scalar(listed_rows[:, t], k.slot[:, 0:CT], parts[:, 1, t:t + 1], wanted[:, t:t + 1],
                                ALU.is_equal, ALU.mult).then_inc(list_ready, 1)
            e.tensor_copy(place_out[:], place_f[:]).then_inc(table_made, 1)

        def sp_places(e, b):
            e.wait_ge(table_made, b + 1)
            with nc.allow_non_contiguous_dma(reason="4 KB of places"):
                e.dma_start(place_dram[b].rearrange("(t p) o -> p (t o)", p=P),
                            place_out[:]).then_inc(table_out, 16)

        def pe_list(e, b):
            e.wait_ge(list_ready, (b + 1) * (2 * NT))
            for t in range(NT):
                ins = e.matmul(list_ps, s.diag[:, t], listed_rows[:, t], start=(t == 0), stop=(t == NT - 1))
            ins.then_inc(listed, 1)

        def dve_list(e, b, first=False):
            e.wait_ge(listed, b + 1)
            if not first:
                e.wait_ge(cx_in, b * (CT * 16))
            e.tensor_copy(ctx_list[:], list_ps).then_inc(list_made, 1)

        def pool_rows(e, b):
            e.wait_ge(list_made, b + 1)
            if b:
                e.wait_ge(cx_turned, b * NQ)
            for r in range(CT):
                e.indirect_dma_start(out=cx[:, r], out_offset=None, in_=a.ctx, element_offset=b * N * FI,
                                     in_offset=bass.IndirectOffsetOnAxis(ap=ctx_list[:, r:r + 1], axis=0)
                                     ).then_inc(cx_in, 16)
            e.wait_ge(table_out, (b + 1) * 16)
            if b:
                e.wait_ge(index_moved, b)
            for t in range(NT):
                e.indirect_dma_start(out=next_index[:, t:t + 1], out_offset=None, in_=place_dram[b],
                                     in_offset=bass.IndirectOffsetOnAxis(ap=twice[:, t:t + 1], axis=0)
                                     ).then_inc(slot_in, 16)

        def dve_move_index(e, b):
            e.wait_ge(slot_in, (b + 1) * (NT * 16))
            e.wait_ge(v.sem, v.value())
            e.tensor_copy(s.index[:], next_index[:]).then_inc(index_moved, 1)

        def dve_bound_weights(e, i):
            part = w0s[0][:, i] if i < KI else w1s[0][:, :, (i - KI) * FO:(i - KI + 1) * FO]
            part = part.bitcast(F32)
            junk = s.products if i < KI else s.products.rearrange("p (c o) -> p c o", c=KD)
            col = Q_W0 + i if i < KI else Q_W1 + i - KI
            done(e.tensor_tensor_reduce(out=junk, in0=part, in1=part, scale=1.0, scalar=0.0, op0=ALU.mult,
                                        op1=ALU.add, accum_out=bounds[:, col:col + 1]))

        def dve_bound_rest(e):
            done(e.tensor_tensor_reduce(out=q[:, 0:H], in0=b0[:], in1=b0[:], scale=1.0, scalar=0.0, op0=ALU.mult,
                                        op1=ALU.add, accum_out=bounds[:, Q_B0:Q_B0 + 1]))
            done(e.tensor_tensor_reduce(out=s.same[0:4 * H], in0=att[:], in1=att[:], scale=1.0, scalar=0.0,
                                        op0=ALU.mult, op1=ALU.add, accum_out=bounds[0:4 * H, Q_A:Q_A + 1]))

        def dve_bounds(e):
            e.wait_ge(att_in, 64)
            dve_bound_rest(e)
            e.wait_ge(cs_squared, B * NT // 2)
            done(e.tensor_reduce(bounds[:, Q_CTX:Q_CTX + 1], ctx_sq[:], AX.X, ALU.max))
            e.tensor_copy(bounds[:, Q_LEAD:Q_LEAD + 1], lead_max[:]).then_inc(bound_made, 1)
            e.wait_ge(bound_spread, 1)
            v.inc(e.reduce_sum(total[:, 0:1], ps[:, 5, 0:P], axis=AX.X))
            done(e.tensor_reduce(total[:, 1:2], ps[:, 5, 0:P], AX.X, ALU.max))
            v.inc(e.tensor_scalar(spread[:, 0], k.ident[:], total[:, 0:1], None, ALU.mult))
            e.tensor_scalar(spread[:, 1], k.ident[:], total[:, 1:2], None, ALU.mult).then_inc(bound_made, 1)

        def dve_verdict(e):
            e.wait_ge(bound_spread, 2)
            done(e.tensor_copy(q[:], ps[:, 5, P:P + 16]))
            sums = ps[:, 5, 0:P]
            squares, root_y, root_t = scratch[:, 0:5], scratch[:, 5:10], scratch[:, 10:15]
            w0, b0n, w1, row, att_norm = (scratch[:, i:i + 1] for i in range(5))
            e0, e1 = scratch[:, 15:16], scratch[:, 16:17]
            v.inc(e.tensor_reduce(w0, sums[:, Q_W0:Q_W0 + KI], AX.X, ALU.add))
            v.inc(e.tensor_copy(b0n, sums[:, Q_B0:Q_B0 + 1]))
            v.inc(e.tensor_reduce(w1, sums[:, Q_W1:Q_W1 + H], AX.X, ALU.max))
            v.inc(e.tensor_copy(row, q[:, Q_CTX:Q_CTX + 1]))
            done(e.tensor_copy(att_norm, q[:, Q_A:Q_A + 1]))
            rsqrt(e, done, squares, root_y, root_t)
            done(e.tensor_tensor(squares, squares, root_y, ALU.mult))
            done(e.tensor_scalar(squares, squares, 1.01, None, ALU.mult))
            done(e.tensor_tensor(e0, row, w0, ALU.mult))
            done(e.tensor_tensor(e1, e0, b0n, ALU.add))
            done(e.tensor_tensor(e1, e1, w1, ALU.mult))
            done(e.tensor_tensor(e0, e0, e1, ALU.add))
            done(e.tensor_tensor(e0, e0, att_norm, ALU.mult))
            done(e.tensor_scalar(e0, e0, 4.0, UNDERFLOW, ALU.mult, ALU.add))
            done(e.tensor_scalar(q[:, Q_LEAD:Q_LEAD + 1], q[:, Q_LEAD:Q_LEAD + 1], 2.0 * ROUNDINGS, None, ALU.add))
            done(e.scalar_tensor_tensor(out=e1, in0=q[:, Q_LEAD:Q_LEAD + 1], scalar=-MASK, in1=e0,
                                        op0=ALU.mult, op1=ALU.add))
            done(e.tensor_scalar(e1, e1, 0.0, None, ALU.is_lt))
            done(e.tensor_scalar(e0, most[:], float(CAP), None, ALU.is_le))
            done(e.tensor_tensor(e1, e1, e0, ALU.mult))
            e.tensor_scalar(flag[:], e1, -1.0, 1.0, ALU.mult, ALU.add).then_inc(bound_made, 1)

        def pe_bounds(e):
            e.wait_ge(bound_made, 1)
            e.matmul(ps[:, 5, 0:P], bounds[:], k.ident[:], start=True, stop=True).then_inc(bound_spread, 1)
            e.wait_ge(bound_made, 2)
            e.matmul(ps[:, 5, 0:P], k.ones[:], spread[:, 0], start=True, stop=True)
            e.matmul(ps[:, 5, P:2 * P], k.ones[:], spread[:, 1], start=True, stop=True).then_inc(bound_spread, 1)

        layers_block = ctx.enter_context(ExitStack())
        block = layers_block.enter_context(nc.Block())

        @block.sync
        def _(e):
            for n in range(4):
                sp_lead(e, n, first=True, par=n)
            for c in range(KI):
                e.dma_start(w0_raw[:, c].rearrange("p (h o) -> p h o", h=H), a.w0[:, c]).then_inc(w_in[0], 16)
            e.wait_ge(b1_zero, 1)
            for row in (0, 32):
                e.dma_start(b1_raw[row:row + 1], a.b1).then_inc(b1_in, 16)
            with nc.allow_non_contiguous_dma(reason="the bias by partition, 4 KB"):
                e.dma_start(b0[:], a.b0.rearrange("h o -> o h")).then_inc(b0_in, 16)
            for n in range(4, NT):
                sp_lead(e, n, par=n % 4)
            for c in range(KD):
                e.dma_start(w1_raw[:, c].rearrange("p (h o) -> p h o", h=H), a.w1[:, c]
                            ).then_inc(w_in[1 + c // (KD // 2)], 16)
                if c == 1:
                    sp_argmax(e, 0)
            s.sp_consts(e)
            sp_places(e, 0)

            def graph(b, first=False, last=False):
                for S in range(SLOTS):
                    if S in LOAD_AT and not last:
                        for t in LOAD_AT[S]:
                            if S or first:
                                sp_lead(e, (b + 1) * NT + t, par=t % 4)
                    if S in SQUARE_AT:
                        sp_square(e, b * (NT // 2) + SQUARE_AT[S], first=first and not SQUARE_AT[S])
                    if S == 0 and first:
                        e.wait_ge(w1_lo, KD)
                        e.wait_ge(w1_hi, KD)
                    if S == 1 and first:
                        s.sp_x(e, 0, first=True)
                    if S == NT // 2 and last:
                        e.wait_ge(l0_made, B * NQ * KD)
                        e.wait_ge(xa_read, B * NT)
                        e.wait_ge(xa_squared, B * NT)
                        s.sp_x(e, b, first=True)
                    if S == ARGMAX_AT and not last:
                        sp_argmax(e, b + 1)
                    if S == ROWS_AT and not last:
                        sp_places(e, b + 1)
                    if not first:
                        for t in BASE_AT.get(S, ()):
                            s.sp_base(e, b - 1, t)
                    if S % 2 and S < SLOTS - 1:
                        sp_rows(e, b, S // 2)
                if b + 2 < B:
                    for t in LOAD_AT[0]:
                        sp_lead(e, (b + 2) * NT + t, par=t % 4)
                sp_rows(e, b, CT - 1)
                if not first and not last:
                    s.sp_x(e, b)
            for b in range(B):
                graph(b, first=b == 0, last=b == B - 1)
            for i, src in enumerate((a.as0, a.an0, a.as1, a.an1)):
                e.dma_start(att[i * H:(i + 1) * H], src).then_inc(att_in, 16)
            for par in y_out:
                e.wait_ge(par, B * (CT // 2 * 16))
            e.wait_ge(cs_squared, B * NT // 2)
            e.wait_ge(s.x1_made[NT - 1], B * 16)
            f.sp(e, first=True)
            for t in range(NT):
                s.sp_base(e, B - 1, t)
            f.sp(e, first=False)

        @block.gpsimd
        def _(e):
            def x1(b):
                for par in y_out:
                    e.wait_ge(par, (b + 1) * (CT // 2 * 16))
                e.wait_ge(index_moved, b + 1)
                s.pool_x1(e, b)

            k.pool(e)
            for b in range(B):
                pool_twice(e, b)
                pool_rows(e, b)
                if b:
                    x1(b - 1)
            x1(B - 1)
            for b in range(B):
                f.pool_tokens(e, b)
            f.pool(e)

        @block.vector
        def _(e):
            v.inc(e.memset(bounds[:], 0.0))
            v.inc(e.memset(lead_max[:], MASK))
            v.inc(e.memset(present[:], 0.0))
            v.inc(e.memset(most[:], 0.0))
            done(e.memset(s.same[:], 0.0))
            e.memset(b1_raw, 0.0).then_inc(b1_zero, 1)
            for row in (0, 32):
                done(e.memset(s.same[row:row + 1], 1.0))
            done(e.tensor_copy(b1_rows[:], s.same[:]))
            k.dve(e)
            for t in range(NT):
                dve_lead(e, 0, t)
            dve_argmax(e, 0, first=True)
            for c in range(KI):
                e.wait_ge(w0_hi, c + 1)
                e.tensor_tensor(w0s[1][:, c], w0_raw[:, c], w0s[0][:, c].bitcast(F32), ALU.subtract).then_inc(w0_lo, 1)
            e.wait_ge(b1_made, 1)
            e.tensor_tensor(b1s[32:33], b1_raw[32:33], b1s[32:33].bitcast(F32), ALU.subtract).then_inc(b1_made, 1)
            e.wait_ge(b1_made, 2)
            dve_leads(e, 0)

            def chunks(g, cs, u):
                for c in cs:
                    dve_layer0(e, g, c, u)
                    if c > cs[0]:
                        dve_low0(e, g, c - 1, u)
                for c in cs[-1:]:
                    dve_low0(e, g, c, u)

            def w1_low(c):
                e.wait_ge(w1_hi, c + 1)
                e.tensor_tensor(w1s[1][:, c], w1_raw[:, c], w1s[0][:, c].bitcast(F32), ALU.subtract).then_inc(w1_lo, 1)
            w1_low(0)
            w1_low(1)
            dve_pairs(e, 0, first=True)
            w1_low(2)
            dve_present(e, 0)
            w1_low(3)
            dve_place(e, 0, first=True)
            w1_low(4)
            dve_list(e, 0, first=True)
            for c in range(5, KD):
                w1_low(c)
            dve_turned(e, 0)
            chunks(0, range(KD), 0)
            s.dve_consts(e)

            def graph(b, first=False, last=False):
                for S in range(SLOTS):
                    tiles = () if first else (TILE_AT_LAST if last else TILE_AT).get(S, ())
                    if S == 0:
                        dve_turned(e, b * NQ + 1)
                    chunks(b * NQ + 1, CHUNKS_G1.get(S, ()), 1)
                    if not last:
                        for t in LEAD_AT.get(S, ()):
                            dve_lead(e, b + 1, t)
                        if S == ARGMAX_AT:
                            dve_argmax(e, b + 1)
                        if S == LEADS_AT:
                            dve_leads(e, b + 1)
                        if S == ROWS_AT:
                            for i, choose in enumerate((dve_pairs, dve_present, dve_place, dve_list)):
                                choose(e, b + 1)
                                for t in tiles[2 * i:2 * i + 2]:
                                    s.dve_tile(e, b - 1, t)
                                if first and i < 3:
                                    for j in range(3 * i, 3 * i + 3):
                                        dve_bound_weights(e, j)
                            tiles = ()
                    for t in tiles:
                        s.dve_tile(e, b - 1, t)
                    if S == NORM_AT - last:
                        if not first:
                            s.dve_norm(e, b - 1)
                        dve_move_index(e, b)
                    if S in CHUNKS_NEXT_G0 and not last:
                        dve_turned(e, b * NQ + 2)
                        chunks(b * NQ + 2, CHUNKS_NEXT_G0[S], 0)
                    if S == RANK_AT - last and not first:
                        for t in range(NT):
                            s.dve_rank(e, b - 1, t)
                        s.dve_onehot(e, b - 1)
                    if first and S == NORM_AT:
                        dve_bound_weights(e, KI + H - 1)
                    if S < NORM_AT:
                        dve_layer1(e, b, S)
                for S in range(NORM_AT, SLOTS):
                    dve_layer1(e, b, S)
                if not first:
                    s.dve_chosen(e, b - 1)
            graph(0, first=True)
            with e.Fori(1, B - 1) as b:
                v.enter(b, 1, LOOP_STEPS)
                graph(b)
                v.leave(B - 2)
            graph(B - 1, last=True)
            for par in y_out:
                e.wait_ge(par, B * (CT // 2 * 16))
            for b in range(B - 1):
                f.dve_tokens(e, b)
            for t in range(NT):
                s.dve_tile(e, B - 1, t)
            e.wait_ge(s.base_made, (B - 1) * NT)
            s.dve_norm(e, B - 1)
            f.dve_turned(e, 0)
            for t in range(NT):
                s.dve_rank(e, B - 1, t)
            s.dve_onehot(e, B - 1)
            for b in range(1, B - 1):
                f.dve_turned(e, b)
            s.dve_chosen(e, B - 1)
            f.dve_tokens(e, B - 1)
            dve_bounds(e)
            f.dve_weights(e)
            f.dve_turned(e, B - 1)
            f.dve(e, beside=dve_verdict)

        @block.scalar
        def _(e):
            def chunks(g, cs, u):
                for c in cs:
                    act_layer0(e, g, c)
                    if c > cs[0]:
                        act_high0(e, g, c - 1, u)
                for c in cs[-1:]:
                    act_high0(e, g, c, u)

            for t in range(4):
                act_squares(e, 0, t)
            e.wait_ge(w_in[0], KI * 16)
            for c in range(KI):
                e.activation(w0s[0][:, c], w0_raw[:, c], ACT.Copy).then_inc(w0_hi, 1)
            e.wait_ge(b1_in, 32)
            e.activation(b1s[:], b1_raw, ACT.Copy).then_inc(b1_made, 1)
            for t in range(4, NT):
                act_squares(e, 0, t)
            for c in range(KD):
                e.wait_ge(w_in[1 + c // (KD // 2)], KD // 2 * 16)
                e.activation(w1s[0][:, c], w1_raw[:, c], ACT.Copy).then_inc(w1_hi, 1)
            act_turned(e, 0, first=True)
            e.wait_ge(b0_in, 16)
            chunks(0, range(KD), 0)

            def graph(b, first=False, last=False):
                for S in range(SLOTS):
                    if S == 0:
                        act_turned(e, b * NQ + 1)
                    chunks(b * NQ + 1, CHUNKS_G1.get(S, ()), 1)
                    if not last:
                        if S == min(CHUNKS_NEXT_G0):
                            act_turned(e, b * NQ + 2)
                        chunks(b * NQ + 2, CHUNKS_NEXT_G0.get(S, ()), 0)
                    if not last and S in LEAD_AT:
                        if S == 0 and not first:
                            e.wait_ge(y_made, b * SLOTS)
                        for t in LEAD_AT[S]:
                            act_squares(e, b + 1, t)
                    if S == RANK_AT and not first:
                        for t in BASE_AT[S]:
                            s.act_base(e, b - 1, t)
                    act_layer1(e, b, S)
                    if S in SQUARE_AT:
                        act_square(e, b * (NT // 2) + SQUARE_AT[S])
                    if S == NORM_AT and not first:
                        for t in BASE_AT[S]:
                            s.act_base(e, b - 1, t)
            over_graphs(e, graph)
            for b in range(B - 1):
                f.act_rows(e, b)
                f.act_turned(e, b)
            for t in range(NT):
                s.act_base(e, B - 1, t)
            f.act_weights(e)
            f.act_rows(e, B - 1)
            f.act_turned(e, B - 1)
            f.act(e)

        @block.tensor
        def _(e):
            def choose(b):
                pe_count(e, b)
                pe_place(e, b)
                pe_list(e, b)

            k.pe(e)
            choose(0)
            pe_turn(e, 0, 0, first=True)
            e.wait_ge(w0_lo, KI)
            for c in range(KD):
                pe_layer0(e, 0, c)
            e.wait_ge(b1_made, 2)
            e.wait_ge(w1_lo, KD)

            def graph(b, first=False, last=False):
                for S in range(SLOTS):
                    if S == 0:
                        pe_turn(e, b, 1)
                    for c in CHUNKS_G1.get(S, ()):
                        pe_layer0(e, b * NQ + 1, c)
                    if not last:
                        if S == min(CHUNKS_NEXT_G0):
                            pe_turn(e, b + 1, 0)
                        for c in CHUNKS_NEXT_G0.get(S, ()):
                            pe_layer0(e, b * NQ + 2, c)
                    if S == NORM_AT and not first:
                        s.pe_spread(e, b - 1)
                    pe_layer1(e, b, S)
                    if S == ROWS_AT and not last:
                        choose(b + 1)
                    if not first:
                        if S == RANK_AT:
                            s.pe_pick(e, b - 1)
            over_graphs(e, graph)
            f.pe_turned(e, 0)
            s.pe_spread(e, B - 1)
            for b in range(1, B - 1):
                f.pe_turned(e, b)
            s.pe_pick(e, B - 1)
            pe_bounds(e)
            f.pe_turned(e, B - 1)
            f.pe(e)

        layers_block.close()

        block = ctx.enter_context(nc.Block())

        @block.gpsimd
        def _(e):
            numbers = sorted(x.num for x in sems)
            while numbers:
                n = 1
                while n < len(numbers) and numbers[n] == numbers[0] + n:
                    n += 1
                e.sem_clear(range(numbers[0], numbers[0] + n))
                numbers = numbers[n:]


def build_full(nc, a, out, flag):
    mask_dram = nc.dram_tensor("mask", (B * N, N), F32, kind="Internal").ap()
    hidden_dram = nc.dram_tensor("hidden", (B * N, D), F32, kind="Internal").ap()
    full_rows = nc.dram_tensor("full_rows", (B * N, D), F32, kind="Internal").ap()

    with ExitStack() as ctx:
        def sem(name, indirect=False):
            return ctx.enter_context(nc.semaphore(name + "_full"))

        def maker(stack):
            return lambda name, shape, dt=F32: stack.enter_context(nc.sbuf_tensor(name + "_full", shape, dt))

        def late(stack, name, shape, dt):
            return stack.enter_context(nc.sbuf_tensor(name + "_full", shape, dt))

        ps = ctx.enter_context(nc.psum_tensor("ps_full", [P, 8, HALF], F32))
        small = maker(ctx)
        k = make_constants(small, sem)
        bn, stats = small("m_bn", [P, 2, 6]), small("m_stats", [P, 2])
        var, rstd, tmp = small("m_var", [P, 1]), small("m_rstd", [P, 1]), small("m_tmp", [P, 1])
        own, top, low = small("own", [P, 1]), small("row_max", [P, 1]), small("row_max_neg", [P, 1])
        total, inverse = small("row_sum", [P, 1]), small("row_inv", [P, 1])
        self_all, neigh_all = small("self_all", [P, NT, H]), small("neigh_all", [P, NT, H])
        self_tile, neigh_tile = small("self_tile", [P, H]), small("neigh_tile", [P, H])
        self_head, neigh_head = small("self_head", [P, NT]), small("neigh_head", [P, NT])
        
        def rows_of(b):
            return full_rows, b * N * D

        s = make_ending(nc, small, small, late, sem, k, a, out, rows_of, ps)
        v, done = s.v, s.done
        with ExitStack() as layers:
            big = maker(layers)
            w = big("w", [P, KD, D])
            a_self, a_neigh, bias = big("a_self", [P, D]), big("a_neigh", [P, D]), big("bias", [P, D])
            rows_in = big("rows_in", [P, D])
            rows_T = big("rows_T", [P, KD, P])
            feat = big("feat", [P, NT * D])
            feat_tile, prod = big("feat_tile", [P, D]), big("prod", [P, D])
            feat_head, bias_head = big("feat_head", [P, NT, P]), big("bias_head", [P, P])
            diag = big("diag_n", [P, NT, P])
            mask, score, prob = big("mask_in", [P, N]), big("score", [P, N]), big("prob", [P, N])
            prob_T = big("prob_T", [P, NT, P])
            mixed, below0, res = big("mixed", [P, FO]), big("below0", [P, FO]), big("res", [P, FO])
        f = make_ffn(nc, maker(ctx), sem, k, s, a, out, rows_of, ps)

        m_in, m_made, m_out, w_in = sem("m_in"), sem("m_made"), sem("m_out"), sem("w_in")
        f_in, f_turned, f_copied, f_made, f_free = (sem("f_" + x) for x in ("in", "turned", "copied", "made", "free"))
        h_diag, h_spread = sem("h_diag"), sem("h_spread")
        t_in, t_scores, t_probs, t_turned, t_copied, t_mixed, t_low, t_exp, t_rows, t_out = (
            sem("t_" + x) for x in ("in", "scores", "probs", "turned", "copied", "mixed", "low", "exp", "rows", "out"))
        index_made = sem("index_made")
        neigh_ps = ps[:, 0:2].rearrange("p a b -> p (a b)")
        turned_ps = ps[:, 2:4].rearrange("p a b -> p (a b)")
        feat_ps = ps[:, 4:6].rearrange("p a b -> p (a b)")
        LAYERS = [
            (KI, a.ctx, a.w0, a.as0, a.an0, a.b0, hidden_dram),
            (KD, hidden_dram, a.w1, a.as1, a.an1, a.b1h, full_rows),
        ]

        def flat(x):
            return x.rearrange("h o -> (h o)").rearrange("(a d) -> a d", a=1).to_broadcast([P, D])

        def loops(e, L, tile, head, row):
            with e.Fori(0, B) as b:
                if tile:
                    with e.Fori(0, NT) as t:
                        tile(b, t, (L * B * NT + b * NT) + t)
                with e.Fori(0, H) as h:
                    n = (L * B * H + b * H) + h
                    if head:
                        head(b, h, n)
                    with e.Fori(0, NT) as t:
                        row(b, h, t, n * NT + t)

        def whenever_flagged(e, program):
            v_flag = e.value_load(flag[0:1, 0:1])
            with e.If(v_flag > 0):
                program(e)
            e.end_ifs()

        block = ctx.enter_context(nc.Block())

        @block.sync
        def _(e):
            def program(e):
                with e.Fori(0, B * NT) as n:
                    e.dma_start(mask[:], a.x[bass.ds(n * P, P), :]).then_inc(m_in, 16)
                    e.wait_ge(m_made, n + 1)
                    e.dma_start(mask_dram[bass.ds(n * P, P), :], score[:]).then_inc(m_out, 16)
                e.wait_ge(m_out, B * NT * 16)
                for L, (K, src, wsrc, asrc, nsrc, bsrc, dst) in enumerate(LAYERS):
                    for c in range(K):
                        e.dma_start(w[:, c].rearrange("p (h o) -> p h o", h=H), wsrc[:, c]).then_inc(w_in, 16)
                    for to, x in ((a_self, asrc), (a_neigh, nsrc), (bias, bsrc)):
                        e.dma_start(to[:], flat(x)).then_inc(w_in, 16)

                    def tile(b, t, n):
                        e.wait_ge(f_free, n + 1)
                        e.dma_start(rows_in[:, 0:K * P], src[bass.ds((b * NT + t) * P, P), :]).then_inc(f_in, 16)

                    def row(b, h, t, n):
                        e.dma_start(mask[:], mask_dram[bass.ds((b * NT + t) * P, P), :]).then_inc(t_in, 16)
                        e.wait_ge(t_rows, n + 1)
                        e.dma_start(dst[bass.ds((b * NT + t) * P, P), bass.ds(h * FO, FO)], res[:]).then_inc(t_out, 16)
                    loops(e, L, tile, None, row)
                    e.wait_ge(t_out, (L + 1) * B * H * NT * 16)
                s.sp_consts(e)

                def graph(b, first=False):
                    s.sp_x(e, b, first)
                    for t in range(NT):
                        s.sp_base(e, b, t)
                graph(0, first=True)
                with e.Fori(1, B) as b:
                    graph(b)
                f.sp(e, first=True)
                f.sp(e, first=False)
            whenever_flagged(e, program)

        @block.gpsimd
        def _(e):
            def program(e):
                k.pool(e)
                for b in range(B):
                    e.wait_ge(index_made, b + 1)
                    s.pool_x1(e, b)
                for b in range(B):
                    f.pool_tokens(e, b)
                f.pool(e)
            whenever_flagged(e, program)

        @block.vector
        def _(e):
            def mask_tile(n):
                e.wait_ge(m_in, (n + 1) * 16)
                for h in range(2):
                    done(e.bn_stats(bn[:, h], mask[:, h * HALF:(h + 1) * HALF]))
                v.inc(e.tensor_copy(top[:], mask[:, 0:1]))
                done(e.bn_aggr(stats[:], bn[:].rearrange("p h s -> p (h s)")))
                done(e.tensor_scalar(var[:], stats[:, 1:2], EPS, None, ALU.add))
                rsqrt(e, done, var[:], rstd[:], tmp[:])
                done(e.tensor_scalar(score[:], mask[:], stats[:, 0:1], rstd[:, 0:1], ALU.subtract, ALU.mult))
                done(e.tensor_scalar(score[:], score[:], -1.0, 1.0, ALU.mult, ALU.add))
                e.tensor_scalar(score[:], score[:], MASK, None, ALU.mult).then_inc(m_made, 1)
                e.wait_ge(m_out, (n + 1) * 16)

            def program(e):
                k.dve(e)
                e.memset(top[:], 0.0).then_inc(f_free, 1)
                e.wait_ge(f_free, 1)
                with e.Fori(0, B * NT) as n:
                    v.enter(n, 0, MASK_STEPS)
                    mask_tile(n)
                    v.leave(B * NT)
                weights = 0
                for L, (K, *_) in enumerate(LAYERS):
                    weights += K + 3
                    e.wait_ge(w_in, weights * 16)

                    def tile(b, t, n):
                        e.wait_ge(f_turned, n + 1)
                        e.tensor_copy(rows_T[:, 0:K].rearrange("p c r -> p (c r)"), turned_ps[:, 0:K * P]
                                      ).then_inc(f_copied, 1)
                        e.wait_ge(f_made, n + 1)
                        done(e.tensor_copy(feat_tile[:], feat_ps))
                        v.inc(e.tensor_copy(feat[:, bass.ds(t * D, D)], feat_tile[:]))
                        for att, tile_sum, all_sums in ((a_self, self_tile, self_all), (a_neigh, neigh_tile, neigh_all)):
                            done(e.tensor_tensor(prod[:], feat_tile[:], att[:], ALU.mult))
                            done(e.tensor_reduce(tile_sum[:], prod[:].rearrange("p (h o) -> p h o", h=H), AX.X,
                                                 ALU.add))
                            done(e.tensor_copy(all_sums[:, bass.ds(t, 1)], tile_sum[:]))
                        e.tensor_copy(top[:], feat_tile[:, 0:1]).then_inc(f_free, 1)
                        e.wait_ge(f_free, n + 2)

                    def head(b, h, n):
                        done(e.tensor_copy(self_head[:], self_all[:, :, bass.ds(h, 1)]))
                        done(e.tensor_copy(neigh_head[:], neigh_all[:, :, bass.ds(h, 1)]))
                        done(e.tensor_copy(bias_head[:], bias[:, bass.ds(h * FO, FO)]))
                        done(e.tensor_copy(feat_head[:], feat[:].rearrange("p (t c) -> p t c", t=NT)
                                           [:, :, bass.ds(h * FO, FO)]))
                        for t in range(NT):
                            ins = e.tensor_scalar(diag[:, t], k.ident[:], neigh_head[:, t:t + 1], None, ALU.mult)
                            if t < NT - 1:
                                done(ins)
                        ins.then_inc(h_diag, 1)

                    def row(b, h, t, n):
                        e.wait_ge(h_spread, (L * B * H + b * H) + h + 1)
                        e.wait_ge(t_in, (n + 1) * 16)
                        done(e.tensor_copy(own[:], self_head[:, bass.ds(t, 1)]))
                        done(e.tensor_scalar(score[:], neigh_ps, own[:, 0:1], None, ALU.add))
                        done(e.scalar_tensor_tensor(out=score[:], in0=score[:], scalar=LRELU, in1=score[:],
                                                    op0=ALU.mult, op1=ALU.max))
                        done(e.tensor_tensor(score[:], score[:], mask[:], ALU.add))
                        done(e.tensor_reduce(top[:], score[:], AX.X, ALU.max))
                        e.tensor_scalar(low[:], top[:], -1.0, None, ALU.mult).then_inc(t_scores, 1)
                        e.wait_ge(t_turned, n + 1)
                        e.tensor_copy(prob_T[:].rearrange("p c r -> p (c r)"), turned_ps).then_inc(t_copied, 1)
                        done(e.reciprocal(inverse[:], total[:]))
                        e.wait_ge(t_mixed, n + 1)
                        done(e.scalar_tensor_tensor(out=mixed[:], in0=ps[:, 6, 0:FO], scalar=inverse[:, 0:1],
                                                    in1=bias_head[:], op0=ALU.mult, op1=ALU.add))
                        e.tensor_scalar(below0[:], mixed[:], 0.0, None, ALU.min).then_inc(t_low, 1)
                        done(e.tensor_scalar(mixed[:], mixed[:], 0.0, None, ALU.max))
                        e.wait_ge(t_exp, n + 1)
                        e.scalar_tensor_tensor(out=res[:], in0=below0[:], scalar=L - 1.0, in1=mixed[:], op0=ALU.add,
                                               op1=ALU.add).then_inc(t_rows, 1)
                        e.wait_ge(t_out, (n + 1) * 16)

                    with e.Fori(0, B) as b:
                        v.enter(b, 0, LAYER_STEPS)
                        with e.Fori(0, NT) as t:
                            v.enter(t, 0, FEAT_STEPS)
                            tile(b, t, (L * B * NT + b * NT) + t)
                            v.leave(NT)
                        with e.Fori(0, H) as h:
                            v.enter(h, 0, HEAD_STEPS + NT * ROW_STEPS)
                            n = (L * B * H + b * H) + h
                            head(b, h, n)
                            assert v.n == HEAD_STEPS, v.n
                            with e.Fori(0, NT) as t:
                                v.enter(t, 0, ROW_STEPS)
                                row(b, h, t, n * NT + t)
                                v.leave(NT)
                            v.leave(H)
                        v.leave(B)
                s.dve_consts(e)

                def graph(b, first=False):
                    if not first:
                        e.wait_ge(index_made, b)
                    e.tensor_copy(s.index[:], k.row[:]).then_inc(index_made, 1)
                    for t in range(NT):
                        s.dve_tile(e, b, t)
                    s.dve_norm(e, b)
                    for t in range(NT):
                        s.dve_rank(e, b, t)
                    s.dve_onehot(e, b)
                    s.dve_chosen(e, b)
                graph(0, first=True)
                with e.Fori(1, B) as b:
                    v.enter(b, 1, END_STEPS)
                    graph(b)
                    v.leave(B - 1)
                e.wait_ge(t_out, 2 * B * H * NT * 16)
                for b in range(B):
                    f.dve_tokens(e, b)
                for b in range(B):
                    f.dve_turned(e, b)
                f.dve_weights(e)
                f.dve(e)
            whenever_flagged(e, program)

        @block.scalar
        def _(e):
            def program(e):
                def row(b, h, t, n):
                    e.wait_ge(t_scores, n + 1)
                    e.activation(prob[:], score[:], ACT.Exp, bias=low[:, 0:1], accum_out=total[:]).then_inc(t_probs, 1)
                    e.wait_ge(t_low, n + 1)
                    e.activation(below0[:], below0[:], ACT.Exp).then_inc(t_exp, 1)
                for L in range(2):
                    loops(e, L, None, None, row)
                with e.Fori(0, B) as b:
                    for t in range(NT):
                        s.act_base(e, b, t)
                for b in range(B):
                    f.act_rows(e, b)
                    f.act_turned(e, b)
                f.act_weights(e)
                f.act(e)
            whenever_flagged(e, program)

        @block.tensor
        def _(e):
            def program(e):
                k.pe(e)
                weights = 0
                for L, (K, *_) in enumerate(LAYERS):
                    weights += K + 3
                    e.wait_ge(w_in, weights * 16)

                    def tile(b, t, n):
                        e.wait_ge(f_in, (n + 1) * 16)
                        for c in range(K):
                            ins = e.transpose(turned_ps[:, c * P:(c + 1) * P], rows_in[:, c * P:(c + 1) * P], k.ident[:])
                        ins.then_inc(f_turned, 1)
                        e.wait_ge(f_copied, n + 1)
                        for h in range(2):
                            for c in range(K):
                                ins = e.matmul(ps[:, 4 + h], rows_T[:, c], w[:, c, h * HALF:(h + 1) * HALF],
                                               start=(c == 0), stop=(c == K - 1))
                        ins.then_inc(f_made, 1)

                    def head(b, h, n):
                        e.wait_ge(h_diag, n + 1)
                        for t in range(NT):
                            ins = e.matmul(neigh_ps[:, t * P:(t + 1) * P], k.ones[:], diag[:, t], start=True, stop=True)
                        ins.then_inc(h_spread, 1)

                    def row(b, h, t, n):
                        e.wait_ge(t_probs, n + 1)
                        for c in range(NT):
                            ins = e.transpose(turned_ps[:, c * P:(c + 1) * P], prob[:, c * P:(c + 1) * P], k.ident[:])
                        ins.then_inc(t_turned, 1)
                        e.wait_ge(t_copied, n + 1)
                        for c in range(NT):
                            ins = e.matmul(ps[:, 6, 0:FO], prob_T[:, c], feat_head[:, c], start=(c == 0),
                                           stop=(c == NT - 1))
                        ins.then_inc(t_mixed, 1)
                    loops(e, L, tile, head, row)
                with e.Fori(0, B) as b:
                    s.pe_spread(e, b)
                    s.pe_pick(e, b)
                for b in range(B):
                    f.pe_turned(e, b)
                f.pe(e)
            whenever_flagged(e, program)


def build(nc, a, out):
    def each_graph(name, shape, dt):
        return [nc.dram_tensor(f"{name}{b}", shape, dt, kind="Internal").ap() for b in range(B)]
    rows_dram = each_graph("layer_rows", (CAP, D), F32)
    argmax_dram, place_dram = each_graph("argmax", (N, 1), U32), each_graph("places", (N, 1), U32)
    with ExitStack() as ctx:
        flag = ctx.enter_context(nc.sbuf_tensor("flag", [P, 1], I32))
        build_lead(nc, ctx, a, out, rows_dram, argmax_dram, place_dram, flag)
        build_full(nc, a, out, flag)


def kernel(**inputs):
    import numpy as _np
    import concourse.bacc as _bacc
    from concourse import mybir as _mybir
    from concourse.bass_utils import run_bass_kernel_spmd as _run

    nc = _bacc.Bacc("TRN2", target_bir_lowering=False, num_devices=1)
    arrays, a = {}, Names()

    def dram(name):
        x = _np.ascontiguousarray(inputs[name])
        arrays[f"in_{name}_dram"] = x
        return nc.dram_tensor(f"in_{name}_dram", x.shape, _mybir.dt.from_np(x.dtype), kind="ExternalInput").ap()

    def by_chunk(w):
        return w.rearrange("h (k p) o -> p k h o", p=P)

    def as_row(w, axes):
        return w.rearrange(f"{axes} -> ({axes})").rearrange("(a d) -> a d", a=1)

    a.x = dram("x").rearrange("b n d -> (b n) d")
    a.ctx = dram("ctx_512").rearrange("b n f -> (b n) f")
    a.w0, a.w1 = by_chunk(dram("L0_xattn_W0")), by_chunk(dram("L0_xattn_W1"))
    a.as0, a.an0, a.b0 = dram("L0_xattn_a_self0"), dram("L0_xattn_a_neigh0"), dram("L0_xattn_b0")
    a.as1, a.an1, a.b1h = dram("L0_xattn_a_self1"), dram("L0_xattn_a_neigh1"), dram("L0_xattn_b1")
    a.b1 = as_row(a.b1h, "h o")
    a.wr, a.br = as_row(dram("L0_ffn_Wr"), "d o"), dram("L0_ffn_br")
    a.fw1, a.fb1 = dram("L0_ffn_W1"), dram("L0_ffn_b1")
    a.fw2, a.fb2 = dram("L0_ffn_W2"), dram("L0_ffn_b2")
    out = nc.dram_tensor("out_0_dram", (B, N, D), F32, kind="ExternalOutput").ap()
    build(nc, a, out.rearrange("b n d -> (b n) d"))
    r = _run(nc, [arrays], core_ids=[0])
    return r.results[0]["out_0_dram"]
```
